# Optimizing a Trainium2 kernel written in Bass

```python
import numpy as np
import jax
import jax.numpy as jnp

def _softmax(x, axis=-1):
    return jax.nn.softmax(x, axis=axis)

def _gelu(x):
    return jax.nn.gelu(x, approximate=True)

def _silu(x):
    return jax.nn.silu(x)

def _sigmoid(x):
    return jax.nn.sigmoid(x)

def _layernorm(x, axis=-1, eps=1e-05):
    m = jnp.mean(x, axis=axis, keepdims=True)
    v = jnp.var(x, axis=axis, keepdims=True)
    return (x - m) / jnp.sqrt(v + eps)

def _scatter_add(tgt, idx, src, axis=0):
    return tgt.at[idx].add(src)

def _segment_sum(src, seg, n):
    return jax.ops.segment_sum(src, seg, n)
kernel_name = 'mk_lm_tower_d1_tok_ids512_r4_a945ba'

def setup_inputs(seed: int=0):
    np.random.seed(seed)
    _w = jnp.asarray

    def _rec_inputs():
        import jax
        import jax.numpy as jnp
        _rk = jax.random.key(seed)
        x = jax.random.randint(jax.random.fold_in(_rk, 1), (16, 128), 0, 128, jnp.int32)
        mask_BS_f1_0 = jnp.where(jnp.ones((16, 128), dtype=bool), 1.0, 0.0).astype(jnp.float32)
        fside_BS_emb = -9.8707e-05 + 0.0200111 * jax.random.normal(jax.random.fold_in(_rk, 22), (16, 128), jnp.float32)
        return (x, mask_BS_f1_0, fside_BS_emb)
    x, mask_BS_f1_0, fside_BS_emb = _rec_inputs()

    def _L0_tok_setup():
        import jax, jax.numpy as jnp
        import numpy as np
        from jax import lax
        B, L, E, H, V, W = (128, 128, 128, 128, 128, 3)
        EPS = 1e-05

        def layer_norm(x, g, b):
            m = jnp.mean(x, axis=-1, keepdims=True)
            v = jnp.mean(jnp.square(x - m), axis=-1, keepdims=True)
            return (x - m) * lax.rsqrt(v + EPS) * g + b
        key = jax.random.key(seed)
        ks = jax.random.split(key, 9)
        input_sequence = jax.random.randint(ks[0], (B, L), 0, V)
        attention_mask = jnp.ones((B, L), jnp.float32)
        emb = jax.random.normal(ks[1], (V, E), jnp.float32) * 0.02
        pos = jax.random.normal(ks[2], (128, E), jnp.float32) * 0.02
        g1 = jnp.ones((E,), jnp.float32)
        b1 = jnp.zeros((E,), jnp.float32)
        conv_w = jax.random.normal(ks[3], (W, E, 2 * H), jnp.float32) * (1.0 / np.sqrt(W * E))
        conv_b = jnp.zeros((2 * H,), jnp.float32)
        g2 = jnp.ones((H,), jnp.float32)
        b2 = jnp.zeros((H,), jnp.float32)
        return dict(input_sequence=input_sequence, attention_mask=attention_mask, emb=emb, pos=pos, g1=g1, b1=b1, conv_w=conv_w, conv_b=conv_b, g2=g2, b2=b2)
    _L0_tok_all = _L0_tok_setup()
    _L0_tok_in = {k: v for k, v in _L0_tok_all.items() if k in ('pos', 'g1', 'b1', 'conv_w', 'conv_b', 'g2', 'b2')}
    del _L0_tok_all

    def _L0_attn_setup():
        import jax, jax.numpy as jnp
        import numpy as np
        Q_THRESH = 0.25
        K_THRESH = 0.25
        V_THRESH = 0.3
        MASK_THRESH = 0.1
        NEG_INF = -1000000000.0

        def _spike(u, threshold):
            return (u >= threshold).astype(u.dtype)
        key = jax.random.key(seed)
        k1, k2, k3, k4 = jax.random.split(key, 4)
        B, L, D = (4, 1024, 128)
        x_seq = jax.random.normal(k1, (B, L, D), dtype=jnp.float32)
        Wq = jax.random.normal(k2, (D, D), dtype=jnp.float32) / np.sqrt(D)
        Wk = jax.random.normal(k3, (D, D), dtype=jnp.float32) / np.sqrt(D)
        Wv = jax.random.normal(k4, (D, D), dtype=jnp.float32) / np.sqrt(D)
        return {'x_seq': x_seq, 'Wq': Wq, 'Wk': Wk, 'Wv': Wv}
    _L0_attn_all = _L0_attn_setup()
    _L0_attn_in = {k: v for k, v in _L0_attn_all.items() if k in ('Wq', 'Wk', 'Wv')}
    del _L0_attn_all

    def _L0_ffn_setup():
        import jax, jax.numpy as jnp
        import numpy as np
        IN_DIM = 128
        HID = 256
        E = 16
        TOPK = 2
        key = jax.random.key(seed)
        ks = jax.random.split(key, 8)
        s = 0.02
        x = jax.random.normal(ks[0], (4, 512, IN_DIM), dtype=jnp.float32)
        Wr = jax.random.normal(ks[1], (IN_DIM, E), dtype=jnp.float32) * s
        br = jnp.zeros((E,), dtype=jnp.float32)
        W1 = jax.random.normal(ks[2], (E, IN_DIM, HID), dtype=jnp.float32) * s
        b1 = jnp.zeros((E, HID), dtype=jnp.float32)
        W2 = jax.random.normal(ks[3], (E, HID, IN_DIM), dtype=jnp.float32) * s
        b2 = jnp.zeros((E, IN_DIM), dtype=jnp.float32)
        return {'x': x, 'Wr': Wr, 'br': br, 'W1': W1, 'b1': b1, 'W2': W2, 'b2': b2}
    _L0_ffn_all = _L0_ffn_setup()
    _L0_ffn_in = {k: v for k, v in _L0_ffn_all.items() if k in ('Wr', 'br', 'W1', 'b1', 'W2', 'b2')}
    del _L0_ffn_all
    return {'x': x, 'mask_BS_f1_0': mask_BS_f1_0, 'fside_BS_emb': fside_BS_emb, 'L0_tok_pos': _L0_tok_in['pos'], 'L0_tok_g1': _L0_tok_in['g1'], 'L0_tok_b1': _L0_tok_in['b1'], 'L0_tok_conv_w': _L0_tok_in['conv_w'], 'L0_tok_conv_b': _L0_tok_in['conv_b'], 'L0_tok_g2': _L0_tok_in['g2'], 'L0_tok_b2': _L0_tok_in['b2'], 'L0_attn_Wq': _L0_attn_in['Wq'], 'L0_attn_Wk': _L0_attn_in['Wk'], 'L0_attn_Wv': _L0_attn_in['Wv'], 'L0_ffn_Wr': _L0_ffn_in['Wr'], 'L0_ffn_br': _L0_ffn_in['br'], 'L0_ffn_W1': _L0_ffn_in['W1'], 'L0_ffn_b1': _L0_ffn_in['b1'], 'L0_ffn_W2': _L0_ffn_in['W2'], 'L0_ffn_b2': _L0_ffn_in['b2']}

def reference(x, mask_BS_f1_0, fside_BS_emb, L0_tok_pos, L0_tok_g1, L0_tok_b1, L0_tok_conv_w, L0_tok_conv_b, L0_tok_g2, L0_tok_b2, L0_attn_Wq, L0_attn_Wk, L0_attn_Wv, L0_ffn_Wr, L0_ffn_br, L0_ffn_W1, L0_ffn_b1, L0_ffn_W2, L0_ffn_b2):
    import jax
    import jax.numpy as jnp

    def _L0_tok_ref(input_sequence, attention_mask, emb, pos, g1, b1, conv_w, conv_b, g2, b2):
        import jax, jax.numpy as jnp
        import numpy as np
        from jax import lax
        B, L, E, H, V, W = (128, 128, 128, 128, 128, 3)
        EPS = 1e-05

        def layer_norm(x, g, b):
            m = jnp.mean(x, axis=-1, keepdims=True)
            v = jnp.mean(jnp.square(x - m), axis=-1, keepdims=True)
            return (x - m) * lax.rsqrt(v + EPS) * g + b
        seq_len = input_sequence.shape[1]
        x = emb[input_sequence] + pos[jnp.arange(seq_len)][None, :, :]
        x = layer_norm(x, g1, b1)
        y = lax.conv_general_dilated(x, conv_w, window_strides=(1,), padding=[(W - 1, W - 1)], dimension_numbers=('NHC', 'HIO', 'NHC')) + conv_b
        a, g = jnp.split(y, 2, axis=-1)
        glu = a * jax.nn.sigmoid(g)
        glu = glu[:, :seq_len, :]
        out = layer_norm(glu + x, g2, b2)
        return out

    def _L0_attn_ref(x_seq, Wq, Wk, Wv):
        import jax, jax.numpy as jnp
        import numpy as np
        Q_THRESH = 0.25
        K_THRESH = 0.25
        V_THRESH = 0.3
        MASK_THRESH = 0.1
        NEG_INF = -1000000000.0

        def _spike(u, threshold):
            return (u >= threshold).astype(u.dtype)
        B, L, D = x_seq.shape
        u_q = jnp.einsum('bld,ed->ble', x_seq, Wq)
        u_k = jnp.einsum('bld,ed->ble', x_seq, Wk)
        u_v = jnp.einsum('bld,ed->ble', x_seq, Wv)
        s_q = _spike(u_q, Q_THRESH)
        s_k = _spike(u_k, K_THRESH)
        s_v = _spike(u_v, V_THRESH)
        score = jnp.einsum('bld,bmd->blm', s_q, s_k)
        causal = jnp.triu(jnp.ones((L, L), dtype=bool), k=1)
        score = jnp.where(causal, NEG_INF, score)
        router_mask = (score > MASK_THRESH).astype(x_seq.dtype)
        out_spike = jnp.einsum('blm,bmd->bld', router_mask, s_v)
        return out_spike

    def _L0_ffn_ref(x, Wr, br, W1, b1, W2, b2):
        import jax, jax.numpy as jnp
        import numpy as np
        IN_DIM = 128
        HID = 256
        E = 16
        TOPK = 2
        token_shape = x.shape[:-1]
        xf = x.reshape(-1, x.shape[-1])
        T = xf.shape[0]
        logits = xf @ Wr + br
        probs = jax.nn.softmax(logits, axis=-1)
        topk_w, topk_idx = jax.lax.top_k(probs, TOPK)
        topk_w = topk_w / jnp.maximum(topk_w.sum(-1, keepdims=True), 1e-09)
        combine = jnp.zeros((T, E), dtype=xf.dtype).at[jnp.arange(T)[:, None], topk_idx].add(topk_w)
        y = jnp.zeros_like(xf)
        for e in range(E):
            h = jax.nn.gelu(xf @ W1[e] + b1[e], approximate=False)
            o = h @ W2[e] + b2[e]
            y = y + combine[:, e:e + 1] * o
        y = xf + y
        return y.reshape(*token_shape, IN_DIM)
    h = _L0_tok_ref(x, mask_BS_f1_0, fside_BS_emb, L0_tok_pos, L0_tok_g1, L0_tok_b1, L0_tok_conv_w, L0_tok_conv_b, L0_tok_g2, L0_tok_b2)
    h = h + _L0_attn_ref(_layernorm(h, axis=-1), L0_attn_Wq, L0_attn_Wk, L0_attn_Wv)
    h = h + _L0_ffn_ref(_layernorm(h, axis=-1), L0_ffn_Wr, L0_ffn_br, L0_ffn_W1, L0_ffn_b1, L0_ffn_W2, L0_ffn_b2)
    return h

_drawn_inputs = setup_inputs


def setup_inputs(seed=0):
    import zlib

    import numpy as np

    out = dict(_drawn_inputs(seed))
    spreads = {'L0_tok_g1': (1.0, 0.2),
     'L0_tok_b1': (0.0, 0.1),
     'L0_tok_conv_b': (0.0, 0.1),
     'L0_tok_g2': (1.0, 0.2),
     'L0_tok_b2': (0.0, 0.1),
     'L0_ffn_br': (0.0, 0.8),
     'L0_ffn_b1': (0.0, 0.8),
     'L0_ffn_b2': (0.0, 2.0)}
    factors = {'L0_ffn_Wr': 8.0, 'L0_ffn_W1': 8.0, 'L0_ffn_W2': 8.0}
    for name, (base, spread) in spreads.items():
        noise = np.random.default_rng([zlib.crc32(name.encode()), seed]).standard_normal(out[name].shape)
        drawn = base * np.exp(spread * noise) if base else spread * noise
        out[name] = jnp.asarray(drawn.astype(out[name].dtype))
    for name, factor in factors.items():
        out[name] = (out[name] * factor).astype(out[name].dtype)
    return out
```

```python
from contextlib import ExitStack

import concourse.bass as bass
from concourse import mybir

F32 = mybir.dt.float32
BF16 = mybir.dt.bfloat16
I32 = mybir.dt.int32
U32 = mybir.dt.uint32
ALU = mybir.AluOpType
ACT = mybir.ActivationFunctionType
AX_X = mybir.AxisListType.X

P = 128
LN_EPS = 1e-5
Q_THRESH = K_THRESH = 0.25
V_THRESH = 0.3
MASK_THRESH = 0.1
TOPK_FLOOR = 1e-9
TOPK = 2
RSQRT_SEED = float(0x5F3759DF)
ROW = 136
ROW_PLACE, ROW_FIRST = 128, 129


def tower_kernel(nc, x, emb, pos, g1, b1, conv_w, conv_b, g2, b2, Wq, Wk, Wv, Wr, br, W1, fb1, W2, fb2, out):
    SEQS, L = x.shape
    ROWS_EMB, D = emb.shape
    TAPS = conv_w.shape[0]
    EXPERTS, _, HID = W1.shape
    assert L == P and D == P and HID == 2 * P
    T = SEQS * L
    GS = 4
    GROUPS = SEQS // GS
    N = GS * L
    PAD = TAPS - 1
    REGION = T + P
    DUMMY = EXPERTS * REGION
    SLOTS = DUMMY + P
    TILES = TOPK * T // P + EXPERTS
    U = 8
    assert TILES % U == 0
    NOWHERE = float(1 << 20)

    slots = nc.dram_tensor("slots", [SLOTS, ROW], F32).ap()
    parts = nc.dram_tensor("parts", [TOPK * T, D], F32).ap()

    with ExitStack() as ctx:
        def sb(name, shape, dt=F32):
            return ctx.enter_context(nc.sbuf_tensor(name, shape, dt))

        def sem(name):
            return ctx.enter_context(nc.semaphore(name))

        bank = [ctx.enter_context(nc.psum_tensor(f"bank{i}", [P, 512], F32)) for i in range(8)]

        ids_i = sb("ids_i", [SEQS, L], I32)
        ids_f = sb("ids_f", [SEQS, 4, L])
        ids_b = sb("ids_b", [SEQS, L], BF16)
        emb_sb = sb("emb_sb", [ROWS_EMB, D])
        pos_sb = sb("pos_sb", [P, D])
        rows4 = sb("rows4", [4, P])
        cols4 = sb("cols4", [P, 4])
        convw_sb = sb("convw_sb", [P, TAPS, 2 * D])
        wqkv = sb("wqkv", [P, 3, D])
        wqkvT = sb("wqkvT", [P, 3, D])
        g2_bc = sb("g2_bc", [P, D])
        b2_bc = sb("b2_bc", [P, D])
        wr_sb = sb("wr_sb", [P, EXPERTS])
        br_bc = sb("br_bc", [P, EXPERTS])
        w1_sb = sb("w1_sb", [P, EXPERTS, HID])
        w2_sb = sb("w2_sb", [P, EXPERTS, 2, D])
        fb1_bc = sb("fb1_bc", [P, EXPERTS, HID])
        fb2_bc = sb("fb2_bc", [P, EXPERTS, D])
        ident = sb("ident", [P, P])
        ident_b = sb("ident_b", [P, P], BF16)
        ones_b = sb("ones_b", [P, P], BF16)
        before_b = sb("before_b", [P, P], BF16)
        causal = sb("causal", [P, P])
        part_id = sb("part_id", [P, 1])
        expert_id = sb("expert_id", [P, EXPERTS])
        region_at = sb("region_at", [P, EXPERTS])
        tile_id = sb("tile_id", [P, TILES])
        zero_rows = sb("zero_rows", [P, ROW])

        onehot = sb("onehot", [ROWS_EMB, GROUPS, N])
        work_a = sb("work_a", [P, GROUPS, N])
        work_b = sb("work_b", [P, GROUPS, N])
        work_c = sb("work_c", [P, GROUPS, N])
        work_d = sb("work_d", [P, GROUPS, N])
        x1T = sb("x1T", [P, GROUPS, GS, PAD + L])
        h0 = sb("h0", [P, GROUPS, N])
        h1 = sb("h1", [P, GROUPS, N])
        spike_q = sb("spike_q", [P, GROUPS, N], BF16)
        spike_k = sb("spike_k", [P, GROUPS, N], BF16)
        spike_v = sb("spike_v", [P, GROUPS, N], BF16)
        routed = sb("routed", [P, GROUPS, N], BF16)
        stage = sb("stage", [P, GROUPS, GS, ROW])
        LNS = 4
        stats = sb("stats", [P, LNS, GROUPS, GS, 6])
        mean_var = sb("mean_var", [P, LNS, GROUPS, GS, 2])
        rs_work = sb("rs_work", [P, LNS, GROUPS, 10, GS])
        probs = sb("probs", [P, GROUPS, 4, GS * EXPERTS])
        row_stat = sb("row_stat", [P, GROUPS, 4, GS])
        top8 = sb("top8", [P, GROUPS, GS, 8])
        top8_at = sb("top8_at", [P, GROUPS, GS, 8], U32)
        top_at = sb("top_at", [P, GROUPS, GS, TOPK])
        chosen = sb("chosen", [P, GROUPS, TOPK, GS * EXPERTS])
        chosen_b = sb("chosen_b", [P, GROUPS, GS * EXPERTS], BF16)
        chosen_sum = sb("chosen_sum", [P, GROUPS + 1, EXPERTS], BF16)
        rank_at = sb("rank_at", [P, GROUPS, 3, GS * EXPERTS])
        slot_of = sb("slot_of", [P, GROUPS, TOPK, GS], I32)
        slot_f = sb("slot_f", [P, GROUPS, TOPK * GS])
        w_work = sb("w_work", [P, GROUPS, 3, GS])
        w_top = sb("w_top", [P, GROUPS, TOPK, GS])

        count_i = sb("count_i", [P, EXPERTS], I32)
        count_up = sb("count_up", [P, EXPERTS], I32)
        tiles_i = sb("tiles_i", [P, EXPERTS], I32)
        tiles_f = sb("tiles_f", [P, EXPERTS])
        zeros_e = sb("zeros_e", [P, EXPERTS])
        tiles_upto = sb("tiles_upto", [P, EXPERTS])
        skip_rows = sb("skip_rows", [P, EXPERTS])
        done_before = sb("done_before", [P, TILES, EXPERTS])
        skipped = sb("skipped", [P, TILES, EXPERTS])
        tile_expert = sb("tile_expert", [P, TILES])
        tile_w = sb("tile_w", [P, TILES], I32)
        tile_skip = sb("tile_skip", [P, TILES])
        tile_row_f = sb("tile_row_f", [P, TILES])
        tile_row = sb("tile_row", [P, TILES], I32)

        xt = sb("xt", [P, U, ROW])
        xtT = sb("xtT", [P, 2, P])
        hid = sb("hid", [P, 2, HID])
        act_h = sb("act_h", [P, 2, HID])
        act_hT = sb("act_hT", [P, 2, HID])
        other = sb("other", [P, U])
        place = sb("place", [P, U], I32)
        y_sb = sb("y_sb", [P, U, D])

        ids_in, emb_in, rows_in, conv_in, qkv_in = map(sem, ("ids_in", "emb_in", "rows_in", "conv_in", "qkv_in"))
        gb2_in, router_in, w1_in, w2_in, fb_in = map(sem, ("gb2_in", "router_in", "w1_in", "w2_in", "fb_in"))
        consts_ready = sem("consts_ready")
        pool_chain, dve_chain, dve_places = sem("pool_chain"), sem("dve_chain"), sem("dve_places")
        ids_ready, ids_spread, onehot_ready = map(sem, ("ids_ready", "ids_spread", "onehot_ready"))
        cols_psum, cols_ready, qkvT_psum, qkvT_ready = map(sem, ("cols_psum", "cols_ready", "qkvT_psum", "qkvT_ready"))
        x0_psum, x0_used = sem("x0_psum"), sem("x0_used")
        ln_ready = [sem(f"ln{i}_ready") for i in range(LNS)]
        normed = [sem(f"normed{i}") for i in range(LNS)]
        xhatT_psum, x1T_ready, convg_psum, conva_psum = map(sem, ("xhatT_psum", "x1T_ready", "convg_psum", "conva_psum"))
        tanh_ready, a_ready, glu_ready, zT_ready, z_psum = map(sem, ("tanh_ready", "a_ready", "glu_ready", "zT_ready", "z_psum"))
        scaled_ready, h0_ready = sem("scaled_ready"), sem("h0_ready")
        xaT_psum, xaT_ready, qkv_psum, spikes_ready = map(sem, ("xaT_psum", "xaT_ready", "qkv_psum", "spikes_ready"))
        score_psum, routed_ready, attn_psum, h1_ready = map(sem, ("score_psum", "routed_ready", "attn_psum", "h1_ready"))
        xfT_psum, xfT_ready, logits_psum = map(sem, ("xfT_psum", "xfT_ready", "logits_psum"))
        shifted_ready, exp_ready, chosen_ready, rank_psum, slots_ready = map(
            sem, ("shifted_ready", "exp_ready", "chosen_ready", "rank_psum", "slots_ready"))
        count_psum, count_ready, table_ready = map(sem, ("count_psum", "count_ready", "table_ready"))
        rows_out, zeros_out, dummy_out = map(sem, ("rows_out", "zeros_out", "dummy_out"))
        xt_in = [sem(f"xt_in{i}") for i in range(U)]
        placed = [sem(f"placed{i}") for i in range(U)]
        t_xT_psum, t_xT, t_h_psum, t_h, t_act, t_actT_psum, t_actT, t_y_psum, t_y, t_place = map(
            sem, ("t_xT_psum", "t_xT", "t_h_psum", "t_h", "t_act", "t_actT_psum", "t_actT", "t_y_psum", "t_y", "t_place"))
        parts_in = [sem(f"parts_in{g}") for g in range(GROUPS)]
        scatters_begun = sem("scatters_begun")
        base_ready, y_out, stored = sem("base_ready"), sem("y_out"), sem("stored")

        def blocks(ap, s):
            return ap[:, s * P:(s + 1) * P]

        def by_seq(ap, n=P):
            return ap.rearrange("p (s n) -> p s n", n=n)

        STAGES = ["x0", "ln0", "xhatT", "conv", "glu", "z", "ln1", "scale", "ln2", "xaT", "qkv",
                  "score", "attn", "ln3", "xfT", "logits", "route", "rank"]
        BEHIND = 4

        def front(program):
            for step in range(len(STAGES) + BEHIND * (GROUPS - 1)):
                for g in range(GROUPS):
                    at = step - BEHIND * g
                    if 0 <= at < len(STAGES) and STAGES[at] in program:
                        program[STAGES[at]](g)

        work = dict(x0=work_a, xhat=work_b, tanh=work_c, a=work_d, glu=work_a, zT=work_b,
                    zhat=work_c, scaled=work_d, xa=work_a, xaT=work_b, xfT=work_c)

        block = ctx.enter_context(nc.Block())

        @block.sync
        def _(sp):
            sp.dma_start(ids_i[:], x).then_inc(ids_in, 16)
            sp.dma_start(emb_sb[:], emb).then_inc(emb_in, 16)
            sp.dma_start(pos_sb[:], pos).then_inc(emb_in, 16)
            for i, row in enumerate((g1, b1, conv_b[0:D], conv_b[D:2 * D])):
                sp.dma_start(rows4[i:i + 1, :], row.rearrange("(o n) -> o n", o=1)).then_inc(rows_in, 16)
            sp.dma_start(convw_sb[:], conv_w.rearrange("w i o -> i w o")).then_inc(conv_in, 16)
            for i, w in enumerate((Wq, Wk, Wv)):
                sp.dma_start(wqkv[:, i, :], w).then_inc(qkv_in, 16)
            sp.dma_start(g2_bc[:], g2.partition_broadcast(P)).then_inc(gb2_in, 16)
            sp.dma_start(b2_bc[:], b2.partition_broadcast(P)).then_inc(gb2_in, 16)
            sp.dma_start(wr_sb[:], Wr).then_inc(router_in, 16)
            sp.dma_start(br_bc[:], br.partition_broadcast(P)).then_inc(router_in, 16)
            sp.dma_start(w1_sb[:], W1.rearrange("e d h -> d e h")).then_inc(w1_in, 16)
            sp.dma_start(w2_sb[:], W2.rearrange("e (c p) d -> p e c d", p=P)).then_inc(w2_in, 16)
            sp.dma_start(fb1_bc[:].rearrange("p e h -> p (e h)"),
                         fb1.rearrange("e h -> (e h)").partition_broadcast(P)).then_inc(fb_in, 16)
            sp.dma_start(fb2_bc[:].rearrange("p e d -> p (e d)"),
                         fb2.rearrange("e d -> (e d)").partition_broadcast(P)).then_inc(fb_in, 16)
            sp.wait_ge(consts_ready, 1)
            sp.dma_start(slots[DUMMY:DUMMY + P, :], zero_rows[:]).then_inc(dummy_out, 16)

            sp.wait_ge(count_ready, 1)
            for e in range(EXPERTS):
                n = sp.value_load(count_i[0:1, e:e + 1], min_val=0, max_val=T)
                sp.dma_start(slots[bass.ds(n + e * REGION, P), :], zero_rows[:]).then_inc(zeros_out, 16)

            sp.wait_ge(table_ready, 1)
            sp.wait_ge(dummy_out, 16)
            sp.wait_ge(zeros_out, 16 * EXPERTS)
            sp.wait_ge(rows_out, 16 * TOPK * SEQS)

            def load(j, u):
                row = sp.value_load(tile_row[0:1, bass.ds(j, 1)], min_val=0, max_val=DUMMY)
                sp.dma_start(xt[:, u, :], slots[bass.ds(row, P), :]).then_inc(xt_in[u], 16)

            for j in range(U):
                load(j, j)
            with sp.Fori(1, TILES // U) as i:
                for u in range(U):
                    sp.wait_ge(t_xT_psum, U * (i - 1) + u + 1)
                    sp.wait_ge(t_place, U * (i - 1) + u + 1)
                    load(U * i + u, u)

            for u in range(U):
                sp.wait_ge(placed[u], 16 * (TILES // U))
            both = parts.rearrange("(k b p) d -> k p b d", k=TOPK, p=P)
            for g in range(GROUPS):
                for k, buf in enumerate((work_a, work_b)):
                    sp.dma_start(by_seq(buf[:, g, :]), both[k, :, g * GS:(g + 1) * GS, :]).then_inc(parts_in[g], 16)
            tokens = out.rearrange("b t d -> t b d")
            for g in range(GROUPS):
                sp.wait_ge(y_out, g + 1)
                sp.dma_start(tokens[:, g * GS:(g + 1) * GS, :], by_seq(work_c[:, g, :])).then_inc(stored, 16)
            sp.wait_ge(stored, 16 * GROUPS)

        @block.gpsimd
        def _(pool):
            done = [0]

            def link(ins):
                done[0] += 1
                ins.then_inc(pool_chain, 1)
                pool.wait_ge(pool_chain, done[0])

            pool.memset(ident[:], 0.0)
            pool.memset(ones_b[:], 1.0)
            pool.memset(zero_rows[:], 0.0)
            pool.memset(zeros_e[:], 0.0)
            pool.memset(causal[:], 1.0)
            pool.memset(stage[:], 0.0)
            pool.memset(chosen_sum[:, 0, :], 0.0)
            link(pool.memset(x1T[:], 0.0))
            link(pool.affine_select(out=ident[:], in_=ident[:], compare_op=ALU.not_equal, fill=1.0, base=0,
                                    pattern=[[-1, P]], channel_multiplier=1))
            pool.affine_select(out=causal[:], in_=causal[:], compare_op=ALU.is_ge, fill=0.0, base=0,
                               pattern=[[1, P]], channel_multiplier=-1)
            pool.affine_select(out=before_b[:], in_=ones_b[:], compare_op=ALU.is_gt, fill=0.0, base=0,
                               pattern=[[1, P]], channel_multiplier=-1)
            pool.iota(part_id[:], pattern=[[0, 1]], base=0, channel_multiplier=1, allow_small_or_imprecise_dtypes=True)
            pool.iota(expert_id[:], pattern=[[1, EXPERTS]], base=0, channel_multiplier=0,
                      allow_small_or_imprecise_dtypes=True)
            pool.iota(region_at[:], pattern=[[REGION, EXPERTS]], base=0, channel_multiplier=0,
                      allow_small_or_imprecise_dtypes=True)
            pool.iota(tile_id[:], pattern=[[1, TILES]], base=0, channel_multiplier=0,
                      allow_small_or_imprecise_dtypes=True)
            pool.iota(stage[:, :, :, ROW_PLACE:ROW_PLACE + 1], pattern=[[N, GROUPS], [P, GS], [0, 1]], base=T,
                      channel_multiplier=1, allow_small_or_imprecise_dtypes=True)
            pool.memset(zero_rows[:, ROW_PLACE:ROW_PLACE + 1], NOWHERE)
            pool.tensor_copy(ident_b[:], ident[:]).then_inc(consts_ready, 1)

            def add_x1(g):
                pool.wait_ge(glu_ready, g + 1)
                pool.tensor_tensor(by_seq(work["zT"][:, g, :]), by_seq(work["glu"][:, g, :]),
                                   x1T[:, g, :, PAD:], ALU.add).then_inc(zT_ready, 1)

            def scale_g2(g):
                if g == 0:
                    pool.wait_ge(gb2_in, 32)
                pool.wait_ge(normed[1], g + 1)
                pool.tensor_tensor(by_seq(work["scaled"][:, g, :]), by_seq(work["zhat"][:, g, :]),
                                   g2_bc[:].unsqueeze(1).broadcast_to([P, GS, D]), ALU.mult).then_inc(scaled_ready, 1)

            def scatter_rows(g):
                pool.wait_ge(slots_ready, g + 1)
                for s in range(GS):
                    for k in range(TOPK):
                        pool.indirect_dma_start(
                            out=slots, out_offset=bass.IndirectOffsetOnAxis(
                                ap=slot_of[:, g, k, s:s + 1].bitcast(U32), axis=0),
                            in_=stage[:, g, s, :], in_offset=None).then_inc(rows_out, 16)

            front(dict(glu=add_x1, scale=scale_g2, rank=scatter_rows))

            last_place = pool.to_reg(TOPK * T - 1)

            def scatter(j, u):
                pool.wait_ge(t_y, j + 1)
                pool.wait_ge(t_place, j + 1)
                pool.sem_inc(scatters_begun, 1)
                pool.indirect_dma_start(
                    out=parts, out_offset=bass.IndirectOffsetOnAxis(ap=place[:, u:u + 1].bitcast(U32), axis=0),
                    in_=y_sb[:, u, :], in_offset=None, bounds_check=last_place,
                    oob_is_err=False).then_inc(placed[u], 16)

            with pool.Fori(0, TILES // U) as i:
                for u in range(U):
                    scatter(U * i + u, u)

        @block.scalar
        def _(act):
            act.wait_ge(cols_psum, 1)
            act.activation(cols4[:, 0:2], bank[7][:, 0:2], ACT.Copy)
            act.activation(cols4[:, 2:4], bank[7][:, 2:4], ACT.Copy, scale=0.5).then_inc(cols_ready, 1)
            act.wait_ge(qkvT_psum, 1)
            act.activation(wqkvT[:].rearrange("p w n -> p (w n)"), bank[6][:, 0:3 * D], ACT.Copy).then_inc(qkvT_ready, 1)
            act.wait_ge(cols_ready, 1)

            def normalise(g, which, src, dst):
                act.wait_ge(ln_ready[which], g + 1)
                for s in range(GS):
                    last = act.activation(dst[s], src[s], ACT.Identity, scale=rs_work[:, which, g, 8, s:s + 1],
                                          bias=rs_work[:, which, g, 9, s:s + 1])
                last.then_inc(normed[which], 1)

            def parts_of(buf, g):
                return [blocks(buf[:, g, :], s) for s in range(GS)]

            def norm_x0(g):
                normalise(g, 0, parts_of(work["x0"], g), parts_of(work["xhat"], g))

            def evacuate_x1T(g):
                act.wait_ge(xhatT_psum, g + 1)
                act.activation(x1T[:, g, :, PAD:], by_seq(bank[0][:]), ACT.Identity, scale=cols4[:, 0:1],
                               bias=cols4[:, 1:2]).then_inc(x1T_ready, 1)

            def gate(g):
                act.wait_ge(convg_psum, g + 1)
                act.activation(work["tanh"][:, g, :], bank[2][:], ACT.Tanh, scale=0.5,
                               bias=cols4[:, 3:4]).then_inc(tanh_ready, 1)
                act.wait_ge(conva_psum, g + 1)
                act.activation(work["a"][:, g, :], bank[3][:], ACT.Identity, scale=0.5,
                               bias=cols4[:, 2:3]).then_inc(a_ready, 1)

            def norm_z(g):
                normalise(g, 1, [blocks(bank[1], s) for s in range(GS)], parts_of(work["zhat"], g))

            def norm_h0(g):
                normalise(g, 2, parts_of(h0, g), parts_of(work["xa"], g))

            def evacuate_xaT(g):
                act.wait_ge(xaT_psum, g + 1)
                act.activation(work["xaT"][:, g, :], bank[1][:], ACT.Copy).then_inc(xaT_ready, 1)

            def norm_h1(g):
                normalise(g, 3, parts_of(h1, g), [stage[:, g, s, 0:D] for s in range(GS)])

            def evacuate_xfT(g):
                act.wait_ge(xfT_psum, g + 1)
                act.activation(work["xfT"][:, g, :], bank[6][:], ACT.Copy).then_inc(xfT_ready, 1)

            def exp_logits(g):
                act.wait_ge(shifted_ready, g + 1)
                act.activation(probs[:, g, 2, :], probs[:, g, 1, :], ACT.Exp).then_inc(exp_ready, 1)

            front(dict(ln0=norm_x0, xhatT=evacuate_x1T, conv=gate, ln1=norm_z, ln2=norm_h0, xaT=evacuate_xaT,
                       ln3=norm_h1, xfT=evacuate_xfT, route=exp_logits))

            def evacuate_x(j, b):
                act.wait_ge(t_xT_psum, j + 1)
                if not isinstance(j, int) or j >= 2:
                    act.wait_ge(t_h_psum, j - 1)
                act.activation(xtT[:, b, :], bank[b][:, 0:P], ACT.Copy).then_inc(t_xT, 1)

            def gelu(j, b):
                act.wait_ge(t_h, j + 1)
                if not isinstance(j, int) or j >= 2:
                    act.wait_ge(t_actT_psum, j - 1)
                act.activation(act_h[:, b, :], hid[:, b, :], ACT.Gelu).then_inc(t_act, 1)

            def evacuate_act(j, b):
                act.wait_ge(t_actT_psum, j + 1)
                if not isinstance(j, int) or j >= 2:
                    act.wait_ge(t_y_psum, j - 1)
                act.activation(act_hT[:, b, :], bank[4 + b][:, 0:HID], ACT.Copy).then_inc(t_actT, 1)

            def step(s, b, static):
                if not static or s < TILES:
                    evacuate_x(s, b)
                if not static or 0 <= s - 3 < TILES:
                    evacuate_act(s - 3, (b + 1) % 2)
                if not static or 0 <= s - 2 < TILES:
                    gelu(s - 2, b)

            for s in range(U):
                step(s, s % 2, True)
            with act.Fori(1, TILES // U) as i:
                for u in range(U):
                    step(U * i + u, u % 2, False)
            for s in range(TILES, TILES + 4):
                step(s, s % 2, True)

        @block.vector
        def _(dve):
            done = [0]

            def link(ins):
                done[0] += 1
                ins.then_inc(dve_chain, 1)
                dve.wait_ge(dve_chain, done[0])

            dve.wait_ge(ids_in, 16)
            link(dve.tensor_scalar(ids_f[:, 0, :], ids_i[:], 0.0, float(ROWS_EMB), ALU.is_lt, ALU.mult))
            link(dve.tensor_tensor(ids_f[:, 1, :], ids_f[:, 0, :], ids_i[:], ALU.add))
            dve.tensor_scalar(ids_b[:], ids_f[:, 1, :], 0.0, float(ROWS_EMB - 1), ALU.max,
                              ALU.min).then_inc(ids_ready, 1)
            dve.wait_ge(consts_ready, 1)
            for g in range(GROUPS):
                dve.wait_ge(ids_spread, g + 1)
                dve.tensor_scalar(onehot[:, g, :], bank[2 + g][0:ROWS_EMB, :], part_id[0:ROWS_EMB, :], None,
                                  ALU.is_equal).then_inc(onehot_ready, 1)

            def rsqrt(g, which):
                w = [rs_work[:, which, g, i, :] for i in range(10)]
                var, mean = mean_var[:, which, g, :, 1], mean_var[:, which, g, :, 0]
                v, y, y2, h, q, z, z2, c = w[:8]
                link(dve.tensor_scalar(v, var, LN_EPS, None, ALU.add))
                link(dve.tensor_scalar(y.bitcast(I32), v.bitcast(I32), -0.5, RSQRT_SEED, ALU.mult, ALU.add))
                link(dve.tensor_tensor(y2, y, y, ALU.mult))
                link(dve.tensor_tensor(h, y2, v, ALU.mult))
                link(dve.scalar_tensor_tensor(out=q, in0=h, scalar=-10 / 3, in1=h, op0=ALU.add, op1=ALU.mult))
                link(dve.scalar_tensor_tensor(out=z, in0=q, scalar=5.0, in1=y, op0=ALU.add, op1=ALU.mult))
                link(dve.tensor_tensor(z2, z, z, ALU.mult))
                link(dve.tensor_tensor(y2, z2, v, ALU.mult))
                link(dve.tensor_scalar(c, y2, -0.5 * 0.375 ** 3, 1.5 * 0.375, ALU.mult, ALU.add))
                link(dve.tensor_tensor(w[8], z, c, ALU.mult))
                dve.scalar_tensor_tensor(out=w[9], in0=mean, scalar=-1.0, in1=w[8], op0=ALU.mult,
                                         op1=ALU.mult).then_inc(ln_ready[which], 1)

            def layer_stats(g, which, src):
                for s in range(GS):
                    last = dve.bn_stats(stats[:, which, g, s, :], blocks(src, s))
                link(last)
                for s in range(GS):
                    last = dve.bn_aggr(mean_var[:, which, g, s, :], stats[:, which, g, s, :])
                link(last)
                rsqrt(g, which)

            def add_pos(g):
                if g == 0:
                    dve.wait_ge(emb_in, 32)
                dve.wait_ge(x0_psum, g + 1)
                x0 = work["x0"][:, g, :]
                link(dve.tensor_tensor(by_seq(x0), by_seq(bank[0][:]), pos_sb[:].unsqueeze(1).broadcast_to([P, GS, D]),
                                       ALU.add))
                layer_stats(g, 0, x0)

            def glu(g):
                dve.wait_ge(tanh_ready, g + 1)
                dve.wait_ge(a_ready, g + 1)
                dve.scalar_tensor_tensor(out=work["glu"][:, g, :], in0=work["tanh"][:, g, :], scalar=1.0,
                                         in1=work["a"][:, g, :], op0=ALU.add, op1=ALU.mult).then_inc(glu_ready, 1)

            def stats_z(g):
                dve.wait_ge(z_psum, g + 1)
                layer_stats(g, 1, bank[1])

            def add_b2(g):
                dve.wait_ge(scaled_ready, g + 1)
                link(dve.tensor_tensor(by_seq(h0[:, g, :]), by_seq(work["scaled"][:, g, :]),
                                       b2_bc[:].unsqueeze(1).broadcast_to([P, GS, D]), ALU.add))
                layer_stats(g, 2, h0[:, g, :])

            def spikes(g):
                dve.wait_ge(qkv_psum, g + 1)
                dve.tensor_scalar(spike_q[:, g, :], bank[4][:], Q_THRESH, None, ALU.is_ge)
                dve.tensor_scalar(spike_k[:, g, :], bank[5][:], K_THRESH, None, ALU.is_ge)
                dve.tensor_scalar(spike_v[:, g, :], bank[6][:], V_THRESH, None, ALU.is_ge).then_inc(spikes_ready, 1)

            def route_mask(g):
                dve.wait_ge(score_psum, g + 1)
                dve.scalar_tensor_tensor(out=by_seq(routed[:, g, :]), in0=by_seq(bank[5][:]), scalar=MASK_THRESH,
                                         in1=causal[:].unsqueeze(1).broadcast_to([P, GS, P]), op0=ALU.is_gt,
                                         op1=ALU.mult).then_inc(routed_ready, 1)

            def add_attn(g):
                dve.wait_ge(attn_psum, g + 1)
                link(dve.tensor_tensor(h1[:, g, :], bank[4][:], h0[:, g, :], ALU.add))
                layer_stats(g, 3, h1[:, g, :])

            def by_expert(ap):
                return ap.rearrange("p (s e) -> p s e", e=EXPERTS)

            def over_experts(ap):
                return ap.unsqueeze(2).broadcast_to([P, GS, EXPERTS])

            def shift_logits(g):
                if g == 0:
                    dve.wait_ge(router_in, 32)
                dve.wait_ge(logits_psum, g + 1)
                logits, shifted = by_expert(probs[:, g, 0, :]), by_expert(probs[:, g, 1, :])
                link(dve.tensor_tensor(logits, by_expert(bank[7][:, 0:GS * EXPERTS]),
                                       br_bc[:].unsqueeze(1).broadcast_to([P, GS, EXPERTS]), ALU.add))
                link(dve.tensor_reduce(row_stat[:, g, 0, :], logits, AX_X, ALU.max))
                dve.tensor_tensor(shifted, logits, over_experts(row_stat[:, g, 0, :]),
                                  ALU.subtract).then_inc(shifted_ready, 1)

            def choose(g):
                dve.wait_ge(exp_ready, g + 1)
                e, p = by_expert(probs[:, g, 2, :]), by_expert(probs[:, g, 3, :])
                link(dve.tensor_reduce(row_stat[:, g, 1, :], e, AX_X, ALU.add))
                link(dve.reciprocal(row_stat[:, g, 2, :], row_stat[:, g, 1, :]))
                link(dve.tensor_tensor(p, e, over_experts(row_stat[:, g, 2, :]), ALU.mult))
                for s in range(GS):
                    last = dve.max(top8[:, g, s, :], p[:, s, :])
                link(last)
                for s in range(GS):
                    last = dve.max_index(top8_at[:, g, s, :], top8[:, g, s, :], p[:, s, :])
                link(last)
                link(dve.tensor_copy(top_at[:, g, :, :], top8_at[:, g, :, 0:TOPK]))
                for k in range(TOPK):
                    last = dve.tensor_tensor(by_expert(chosen[:, g, k, :]),
                                             expert_id[:].unsqueeze(1).broadcast_to([P, GS, EXPERTS]),
                                             over_experts(top_at[:, g, :, k]), ALU.is_equal)
                link(last)
                dve.tensor_tensor(chosen_b[:, g, :], chosen[:, g, 0, :], chosen[:, g, 1, :],
                                  ALU.add).then_inc(chosen_ready, 1)
                link(dve.tensor_tensor(w_work[:, g, 0, :], top8[:, g, :, 0], top8[:, g, :, 1], ALU.add))
                link(dve.tensor_scalar(w_work[:, g, 1, :], w_work[:, g, 0, :], TOPK_FLOOR, None, ALU.max))
                link(dve.reciprocal(w_work[:, g, 2, :], w_work[:, g, 1, :]))
                for k in range(TOPK):
                    dve.tensor_tensor(w_top[:, g, k, :], top8[:, g, :, k], w_work[:, g, 2, :], ALU.mult)
                counts = chosen_b[:, g, :].rearrange("p (s e) -> p e s", e=EXPERTS)
                link(dve.tensor_reduce(rank_at[:, g, 2, 0:EXPERTS], counts, AX_X, ALU.add))
                dve.tensor_tensor(chosen_sum[:, g + 1, :], rank_at[:, g, 2, 0:EXPERTS], chosen_sum[:, g, :],
                                  ALU.add).then_inc(chosen_ready, 1)

            def slots_of(g):
                dve.wait_ge(rank_psum, g + 1)
                at = by_expert(rank_at[:, g, 0, :])
                link(dve.tensor_tensor(at, by_expert(bank[7][:, 64:64 + GS * EXPERTS]),
                                       region_at[:].unsqueeze(1).broadcast_to([P, GS, EXPERTS]), ALU.add))
                link(dve.tensor_tensor(rank_at[:, g, 1:3, :], chosen[:, g, :, :],
                                       rank_at[:, g, 0:1, :].broadcast_to([P, TOPK, GS * EXPERTS]), ALU.mult))
                link(dve.tensor_reduce(slot_f[:, g, :], rank_at[:, g, 1:3, :].rearrange("p k (s e) -> p (k s) e", e=EXPERTS),
                                       AX_X, ALU.add))
                dve.tensor_copy(slot_of[:, g, :, :].rearrange("p k s -> p (k s)"), slot_f[:, g, :])
                dve.wait_ge(normed[3], g + 1)
                dve.tensor_copy(stage[:, g, :, ROW_FIRST], top_at[:, g, :, 0]).then_inc(slots_ready, 1)

            front(dict(x0=add_pos, glu=glu, z=stats_z, scale=add_b2, qkv=spikes, score=route_mask, attn=add_attn,
                       logits=shift_logits, route=choose, rank=slots_of))

            dve.wait_ge(count_psum, 1)
            dve.tensor_copy(count_i[:], bank[7][:, 128:128 + EXPERTS]).then_inc(count_ready, 1)
            link(dve.tensor_scalar(count_up[:], bank[7][:, 128:128 + EXPERTS], float(P - 1), None, ALU.add))
            link(dve.tensor_scalar(tiles_i[:], count_up[:], P.bit_length() - 1, None, ALU.logical_shift_right))
            link(dve.tensor_copy(tiles_f[:], tiles_i[:]))
            dve.tensor_scalar(skip_rows[:], tiles_f[:], -float(P), float(REGION), ALU.mult, ALU.add)
            link(dve.tensor_tensor_scan(tiles_upto[:], tiles_f[:], zeros_e[:], 0.0, ALU.add, ALU.add))
            every = [P, TILES, EXPERTS]
            link(dve.tensor_tensor(done_before[:], tile_id[:].unsqueeze(2).broadcast_to(every),
                                   tiles_upto[:].unsqueeze(1).broadcast_to(every), ALU.is_ge))
            dve.tensor_tensor(skipped[:], done_before[:], skip_rows[:].unsqueeze(1).broadcast_to(every), ALU.mult)
            link(dve.tensor_reduce(tile_expert[:], done_before[:], AX_X, ALU.add))
            link(dve.tensor_reduce(tile_skip[:], skipped[:], AX_X, ALU.add))
            dve.tensor_scalar(tile_w[:], tile_expert[:], float(EXPERTS - 1), None, ALU.min)
            link(dve.scalar_tensor_tensor(out=tile_row_f[:], in0=tile_id[:], scalar=float(P), in1=tile_skip[:],
                                          op0=ALU.mult, op1=ALU.add))
            dve.tensor_scalar(tile_row[:], tile_row_f[:], float(DUMMY), None, ALU.min).then_inc(table_ready, 1)

            for g in range(GROUPS):
                last = dve.tensor_tensor(by_seq(h0[:, g, :]), by_seq(h1[:, g, :]), stage[:, g, :, 0:D], ALU.add)
            last.then_inc(base_ready, 1)

            dve.wait_ge(table_ready, 1)
            dve.wait_ge(fb_in, 32)

            def expert_of(j):
                return dve.value_load(tile_w[0:1, bass.ds(j, 1)], min_val=0, max_val=EXPERTS - 1)

            def add_b1(j, b):
                e = expert_of(j)
                dve.wait_ge(t_h_psum, j + 1)
                if not isinstance(j, int) or j >= 2:
                    dve.wait_ge(t_act, j - 1)
                dve.tensor_tensor(hid[:, b, :], bank[2 + b][:, 0:HID],
                                  fb1_bc[:, bass.ds(e, 1), :].rearrange("p o h -> p (o h)"), ALU.add).then_inc(t_h, 1)

            def places(j, u, lap):
                dve.wait_ge(xt_in[u], 16 * (lap + 1))
                if not isinstance(lap, int) or lap >= 1:
                    dve.wait_ge(placed[u], 16 * lap)
                dve.tensor_scalar(other[:, u:u + 1], xt[:, u, ROW_FIRST:ROW_FIRST + 1],
                                  tile_expert[:, bass.ds(j, 1)], -float(T), ALU.is_equal,
                                  ALU.mult).then_inc(dve_places, 1)
                dve.wait_ge(dve_places, j + 1)
                dve.tensor_tensor(place[:, u:u + 1], other[:, u:u + 1], xt[:, u, ROW_PLACE:ROW_PLACE + 1],
                                  ALU.add).then_inc(t_place, 1)

            def add_b2(j, u, lap):
                e = expert_of(j)
                dve.wait_ge(t_y_psum, j + 1)
                if not isinstance(lap, int) or lap >= 1:
                    dve.wait_ge(placed[u], 16 * lap)
                dve.tensor_tensor(y_sb[:, u, :], bank[6 + u % 2][:, 0:D],
                                  fb2_bc[:, bass.ds(e, 1), :].rearrange("p o h -> p (o h)"), ALU.add).then_inc(t_y, 1)

            def step(s, u, lap, static):
                if not static or 0 <= s - 1 < TILES:
                    add_b1(s - 1, (u + 1) % 2)
                if not static or s < TILES:
                    places(s, u, lap)
                if not static or 0 <= s - 4 < TILES:
                    add_b2(s - 4, (u - 4) % U, lap if u >= 4 else lap - 1)

            for s in range(U):
                step(s, s % U, s // U, True)
            with dve.Fori(1, TILES // U) as i:
                for u in range(U):
                    step(U * i + u, u, i, False)
            for s in range(TILES, TILES + 4):
                step(s, s % U, s // U, True)

            for g in range(GROUPS):
                dve.wait_ge(parts_in[g], 32)
                for s in range(GS):
                    link_last = dve.scalar_tensor_tensor(
                        out=blocks(work_d[:, g, :], s), in0=blocks(work_a[:, g, :], s), scalar=w_top[:, g, 0, s:s + 1],
                        in1=blocks(h0[:, g, :], s), op0=ALU.mult, op1=ALU.add)
                link(link_last)
                for s in range(GS):
                    last = dve.scalar_tensor_tensor(
                        out=blocks(work_c[:, g, :], s), in0=blocks(work_b[:, g, :], s), scalar=w_top[:, g, 1, s:s + 1],
                        in1=blocks(work_d[:, g, :], s), op0=ALU.mult, op1=ALU.add)
                last.then_inc(y_out, 1)

        @block.tensor
        def _(pe):
            pe.wait_ge(consts_ready, 1)
            pe.wait_ge(ids_ready, 1)
            for g in range(GROUPS):
                for s in range(GS):
                    b = g * GS + s
                    last = pe.matmul(blocks(bank[2 + g][0:ROWS_EMB, :], s),
                                     ident_b[0:SEQS, b:b + 1].broadcast_to([SEQS, ROWS_EMB]), ids_b[:],
                                     start=True, stop=True)
                last.then_inc(ids_spread, 1)
            pe.wait_ge(rows_in, 64)
            pe.transpose(bank[7][:, 0:4], rows4[:], ident[0:4, 0:4]).then_inc(cols_psum, 1)
            pe.wait_ge(qkv_in, 48)
            pe.wait_ge(onehot_ready, GROUPS)
            for i in range(3):
                last = pe.transpose(bank[6][:, i * D:(i + 1) * D], wqkv[:, i, :], ident[:])
            last.then_inc(qkvT_psum, 1)

            def turn(dst, src):
                for s in range(GS):
                    last = pe.transpose(blocks(dst, s), src[s], ident[:])
                return last

            def parts_of(buf, g):
                return [blocks(buf[:, g, :], s) for s in range(GS)]

            def lookup(g):
                if g == 0:
                    pe.wait_ge(emb_in, 32)
                pe.wait_ge(onehot_ready, g + 1)
                if g >= 1:
                    pe.wait_ge(x1T_ready, g)
                for s in range(GS):
                    last = pe.matmul(blocks(bank[0], s), blocks(onehot[:, g, :], s), emb_sb[:], start=True, stop=True)
                last.then_inc(x0_psum, 1)

            def turn_xhat(g):
                pe.wait_ge(normed[0], g + 1)
                turn(bank[0], parts_of(work["xhat"], g)).then_inc(xhatT_psum, 1)

            def conv(g):
                if g == 0:
                    pe.wait_ge(conv_in, 16)
                pe.wait_ge(x1T_ready, g + 1)
                for half, acc, free, full in ((1, bank[2], tanh_ready, convg_psum), (0, bank[3], a_ready, conva_psum)):
                    if g >= 1:
                        pe.wait_ge(free, g)
                    for w in range(TAPS):
                        last = pe.matmul(by_seq(acc[:]), convw_sb[:, w, half * D:(half + 1) * D],
                                         x1T[:, g, :, w:w + L], start=(w == 0), stop=(w == TAPS - 1))
                    last.then_inc(full, 1)

            def turn_z(g):
                pe.wait_ge(zT_ready, g + 1)
                if g >= 1:
                    pe.wait_ge(xaT_ready, g)
                turn(bank[1], parts_of(work["zT"], g)).then_inc(z_psum, 1)

            def turn_xa(g):
                pe.wait_ge(normed[2], g + 1)
                turn(bank[1], parts_of(work["xa"], g)).then_inc(xaT_psum, 1)

            def project(g):
                if g == 0:
                    pe.wait_ge(qkvT_ready, 1)
                pe.wait_ge(xaT_ready, g + 1)
                if g >= 1:
                    pe.wait_ge(ln_ready[3], g)
                    pe.wait_ge(xfT_ready, g)
                xaT = work["xaT"][:, g, :]
                pe.matmul(bank[4][:], wqkvT[:, 0, :], xaT, start=True, stop=True)
                pe.matmul(bank[5][:], wqkvT[:, 1, :], xaT, start=True, stop=True)
                for s in range(GS):
                    last = pe.matmul(blocks(bank[6], s), blocks(xaT, s), wqkvT[:, 2, :], start=True, stop=True)
                last.then_inc(qkv_psum, 1)

            def score(g):
                pe.wait_ge(spikes_ready, g + 1)
                for s in range(GS):
                    last = pe.matmul(blocks(bank[5], s), blocks(spike_k[:, g, :], s), blocks(spike_q[:, g, :], s),
                                     start=True, stop=True)
                last.then_inc(score_psum, 1)

            def attend(g):
                pe.wait_ge(routed_ready, g + 1)
                for s in range(GS):
                    last = pe.matmul(blocks(bank[4], s), blocks(routed[:, g, :], s), blocks(spike_v[:, g, :], s),
                                     start=True, stop=True)
                last.then_inc(attn_psum, 1)

            def turn_xf(g):
                pe.wait_ge(normed[3], g + 1)
                turn(bank[6], [stage[:, g, s, 0:D] for s in range(GS)]).then_inc(xfT_psum, 1)

            def router(g):
                if g == 0:
                    pe.wait_ge(router_in, 32)
                pe.wait_ge(xfT_ready, g + 1)
                if g >= 1:
                    pe.wait_ge(slots_ready, g)
                for s in range(GS):
                    last = pe.matmul(bank[7][:, s * EXPERTS:(s + 1) * EXPERTS], blocks(work["xfT"][:, g, :], s),
                                     wr_sb[:], start=True, stop=True)
                last.then_inc(logits_psum, 1)

            def rank(g):
                pe.wait_ge(chosen_ready, 2 * g + 2)
                ranks = bank[7][:, 64:64 + GS * EXPERTS]
                pe.matmul(ranks, before_b[:], chosen_b[:, g, :], start=True, stop=False)
                for s in range(GS - 1):
                    behind = GS - 1 - s
                    pe.matmul(ranks[:, (s + 1) * EXPERTS:].rearrange("p (s e) -> p s e", e=EXPERTS), ones_b[:],
                              chosen_b[:, g, s * EXPERTS:(s + 1) * EXPERTS].unsqueeze(1)
                              .broadcast_to([P, behind, EXPERTS]), start=False, stop=False)
                pe.matmul(ranks.rearrange("p (s e) -> p s e", e=EXPERTS), ones_b[:],
                          chosen_sum[:, g, :].unsqueeze(1).broadcast_to([P, GS, EXPERTS]),
                          start=False, stop=True).then_inc(rank_psum, 1)
                if g == GROUPS - 1:
                    pe.wait_ge(slots_ready, GROUPS)
                    pe.matmul(bank[7][:, 128:128 + EXPERTS], ones_b[:], chosen_sum[:, GROUPS, :],
                              start=True, stop=True).then_inc(count_psum, 1)

            front(dict(x0=lookup, xhatT=turn_xhat, conv=conv, z=turn_z, xaT=turn_xa, qkv=project, score=score,
                       attn=attend, xfT=turn_xf, logits=router, rank=rank))

            pe.wait_ge(table_ready, 1)
            pe.wait_ge(w1_in, 16)
            pe.wait_ge(w2_in, 16)

            def expert_of(j):
                return pe.value_load(tile_w[0:1, bass.ds(j, 1)], min_val=0, max_val=EXPERTS - 1)

            def turn_x(j, u, lap):
                pe.wait_ge(xt_in[u], 16 * (lap + 1))
                if not isinstance(j, int) or j >= 2:
                    pe.wait_ge(t_xT, j - 1)
                pe.transpose(bank[u % 2][:, 0:P], xt[:, u, 0:D], ident[:]).then_inc(t_xT_psum, 1)

            def first(j, b):
                e = expert_of(j)
                pe.wait_ge(t_xT, j + 1)
                if not isinstance(j, int) or j >= 2:
                    pe.wait_ge(t_h, j - 1)
                pe.matmul(bank[2 + b][:, 0:HID], xtT[:, b, :], w1_sb[:, bass.ds(e, 1), :].rearrange("p o h -> p (o h)"),
                          start=True, stop=True).then_inc(t_h_psum, 1)

            def turn_act(j, b):
                pe.wait_ge(t_act, j + 1)
                if not isinstance(j, int) or j >= 2:
                    pe.wait_ge(t_actT, j - 1)
                for c in range(2):
                    last = pe.transpose(bank[4 + b][:, c * P:(c + 1) * P], act_h[:, b, c * P:(c + 1) * P], ident[:])
                last.then_inc(t_actT_psum, 1)

            def second(j, b):
                e = expert_of(j)
                pe.wait_ge(t_actT, j + 1)
                if not isinstance(j, int) or j >= 2:
                    pe.wait_ge(t_y, j - 1)
                for c in range(2):
                    last = pe.matmul(bank[6 + b][:, 0:D], act_hT[:, b, c * P:(c + 1) * P],
                                     w2_sb[:, bass.ds(e, 1), c, :].rearrange("p o h -> p (o h)"),
                                     start=(c == 0), stop=(c == 1))
                last.then_inc(t_y_psum, 1)

            def step(s, u, lap, static):
                if not static or s < TILES:
                    turn_x(s, u, lap)
                if not static or 0 <= s - 4 < TILES:
                    second(s - 4, u % 2)
                if not static or 0 <= s - 1 < TILES:
                    first(s - 1, (u + 1) % 2)
                if not static or 0 <= s - 3 < TILES:
                    turn_act(s - 3, (u + 1) % 2)

            for s in range(U):
                step(s, s % U, s // U, True)
            with pe.Fori(1, TILES // U) as i:
                for u in range(U):
                    step(U * i + u, u, i, False)
            for s in range(TILES, TILES + 4):
                step(s, s % U, s // U, True)


_INS = ["x", "fside_BS_emb", "L0_tok_pos", "L0_tok_g1", "L0_tok_b1", "L0_tok_conv_w", "L0_tok_conv_b", "L0_tok_g2",
        "L0_tok_b2", "L0_attn_Wq", "L0_attn_Wk", "L0_attn_Wv", "L0_ffn_Wr", "L0_ffn_br", "L0_ffn_W1", "L0_ffn_b1",
        "L0_ffn_W2", "L0_ffn_b2"]


def kernel(**inputs):
    import numpy as _np
    import concourse.bacc as _bacc
    from concourse import mybir as _mybir
    from concourse.bass_utils import run_bass_kernel_spmd as _run

    nc = _bacc.Bacc("TRN2", target_bir_lowering=False, num_devices=1)
    arrays, args = {}, []
    for name in _INS:
        a = _np.ascontiguousarray(inputs[name])
        arrays[f"in_{name}_dram"] = a
        args.append(nc.dram_tensor(f"in_{name}_dram", a.shape, _mybir.dt.from_np(a.dtype), kind="ExternalInput").ap())
    args.append(nc.dram_tensor("out_0_dram", (16, 128, 128), _mybir.dt.float32, kind="ExternalOutput").ap())
    tower_kernel(nc, *args)
    r = _run(nc, [arrays], core_ids=[0])
    return r.results[0]["out_0_dram"]
```

```python
from contextlib import ExitStack

import concourse.bass as bass
from concourse import mybir

F32 = mybir.dt.float32
BF16 = mybir.dt.bfloat16
I32 = mybir.dt.int32
U32 = mybir.dt.uint32
ALU = mybir.AluOpType
ACT = mybir.ActivationFunctionType
AX_X = mybir.AxisListType.X

P = 128
LN_EPS = 1e-5
Q_THRESH = K_THRESH = 0.25
V_THRESH = 0.3
MASK_THRESH = 0.1
TOPK_FLOOR = 1e-9
TOPK = 2
RSQRT_SEED = float(0x5F3759DF)
ROW = 136
ROW_PLACE, ROW_FIRST = 128, 129


def tower_kernel(nc, x, emb, pos, g1, b1, conv_w, conv_b, g2, b2, Wq, Wk, Wv, Wr, br, W1, fb1, W2, fb2, out):
    SEQS, L = x.shape
    ROWS_EMB, D = emb.shape
    TAPS = conv_w.shape[0]
    EXPERTS, _, HID = W1.shape
    assert L == P and D == P and HID == 2 * P
    T = SEQS * L
    GS = 4
    GROUPS = SEQS // GS
    N = GS * L
    PAD = TAPS - 1
    REGION = T + P
    DUMMY = EXPERTS * REGION
    SLOTS = DUMMY + P
    FULL = TOPK * T // P
    TILES = FULL + EXPERTS
    U = 8
    assert FULL % U == 0 and TILES % U == 0
    NOWHERE = float(1 << 20)

    slots = nc.dram_tensor("slots", [SLOTS, ROW], F32).ap()
    parts = nc.dram_tensor("parts", [TOPK * T, D], F32).ap()

    with ExitStack() as ctx:
        def sb(name, shape, dt=F32):
            return ctx.enter_context(nc.sbuf_tensor(name, shape, dt))

        def sem(name):
            return ctx.enter_context(nc.semaphore(name))

        bank = [ctx.enter_context(nc.psum_tensor(f"bank{i}", [P, 512], F32)) for i in range(8)]

        ids_i = sb("ids_i", [SEQS, L], I32)
        ids_f = sb("ids_f", [SEQS, 4, L])
        ids_b = sb("ids_b", [SEQS, L], BF16)
        emb_sb = sb("emb_sb", [ROWS_EMB, D])
        pos_sb = sb("pos_sb", [P, D])
        rows4 = sb("rows4", [4, P])
        cols4 = sb("cols4", [P, 4])
        convw_sb = sb("convw_sb", [P, TAPS, 2 * D])
        wqkv = sb("wqkv", [P, 3, D])
        wqkvT = sb("wqkvT", [P, 3, D])
        g2_bc = sb("g2_bc", [P, D])
        b2_bc = sb("b2_bc", [P, D])
        wr_sb = sb("wr_sb", [P, EXPERTS])
        br_bc = sb("br_bc", [P, EXPERTS])
        w1_sb = sb("w1_sb", [P, EXPERTS, HID])
        w2_sb = sb("w2_sb", [P, EXPERTS, 2, D])
        fb1_bc = sb("fb1_bc", [P, EXPERTS, HID])
        fb2_bc = sb("fb2_bc", [P, EXPERTS, D])
        ident = sb("ident", [P, P])
        ident_b = sb("ident_b", [P, P], BF16)
        ones_b = sb("ones_b", [P, P], BF16)
        before_b = sb("before_b", [P, P], BF16)
        causal = sb("causal", [P, P])
        part_id = sb("part_id", [P, 1])
        expert_id = sb("expert_id", [P, EXPERTS])
        region_at = sb("region_at", [P, EXPERTS])
        tile_id = sb("tile_id", [P, FULL])
        zero_rows = sb("zero_rows", [P, ROW])

        onehot = sb("onehot", [ROWS_EMB, GROUPS, N])
        work_a = sb("work_a", [P, GROUPS, N])
        work_b = sb("work_b", [P, GROUPS, N])
        work_c = sb("work_c", [P, GROUPS, N])
        work_d = sb("work_d", [P, GROUPS, N])
        x1T = sb("x1T", [P, GROUPS, GS, PAD + L])
        h0 = sb("h0", [P, GROUPS, N])
        h1 = sb("h1", [P, GROUPS, N])
        spike_q = sb("spike_q", [P, GROUPS, N], BF16)
        spike_k = sb("spike_k", [P, GROUPS, N], BF16)
        spike_v = sb("spike_v", [P, GROUPS, N], BF16)
        routed = sb("routed", [P, GROUPS, N], BF16)
        stage = sb("stage", [P, GROUPS, GS, ROW])
        LNS = 4
        stats = sb("stats", [P, LNS, GROUPS, GS, 6])
        mean_var = sb("mean_var", [P, LNS, GROUPS, GS, 2])
        rs_work = sb("rs_work", [P, LNS, GROUPS, 10, GS])
        probs = sb("probs", [P, GROUPS, 4, GS * EXPERTS])
        row_stat = sb("row_stat", [P, GROUPS, 4, GS])
        top8 = sb("top8", [P, GROUPS, GS, 8])
        top8_at = sb("top8_at", [P, GROUPS, GS, 8], U32)
        top_at = sb("top_at", [P, GROUPS, GS, TOPK])
        chosen = sb("chosen", [P, GROUPS, TOPK, GS * EXPERTS])
        chosen_b = sb("chosen_b", [P, GROUPS, GS * EXPERTS], BF16)
        chosen_sum = sb("chosen_sum", [P, GROUPS + 1, EXPERTS], BF16)
        rank_at = sb("rank_at", [P, GROUPS, 3, GS * EXPERTS])
        slot_of = sb("slot_of", [P, GROUPS, TOPK, GS], I32)
        slot_f = sb("slot_f", [P, GROUPS, TOPK * GS])
        w_work = sb("w_work", [P, GROUPS, 3, GS])
        w_top = sb("w_top", [P, GROUPS, TOPK, GS])

        count_i = sb("count_i", [P, EXPERTS], I32)
        tiles_i = sb("tiles_i", [P, EXPERTS], I32)
        tiles_f = sb("tiles_f", [P, EXPERTS])
        zeros_e = sb("zeros_e", [P, EXPERTS])
        tiles_upto = sb("tiles_upto", [P, EXPERTS])
        skip_rows = sb("skip_rows", [P, EXPERTS])
        done_before = sb("done_before", [P, FULL, EXPERTS])
        skipped = sb("skipped", [P, FULL, EXPERTS])
        tile_expert = sb("tile_expert", [P, FULL])
        tile_w = sb("tile_w", [P, FULL], I32)
        tile_skip = sb("tile_skip", [P, FULL])
        tile_row_f = sb("tile_row_f", [P, FULL])
        tile_row = sb("tile_row", [P, FULL], I32)
        tail_row = sb("tail_row", [P, EXPERTS], I32)

        xt = sb("xt", [P, U, ROW])
        xtT = sb("xtT", [P, 2, P])
        hid = sb("hid", [P, 2, HID])
        act_h = sb("act_h", [P, 2, HID])
        act_hT = sb("act_hT", [P, 2, HID])
        other = sb("other", [P, U])
        place = sb("place", [P, U], I32)
        y_sb = sb("y_sb", [P, U, D])

        ids_in, emb_in, rows_in, conv_in, qkv_in = map(sem, ("ids_in", "emb_in", "rows_in", "conv_in", "qkv_in"))
        gb2_in, router_in, w1_in, w2_in, fb_in = map(sem, ("gb2_in", "router_in", "w1_in", "w2_in", "fb_in"))
        consts_ready = sem("consts_ready")
        pool_chain, dve_chain, dve_places = sem("pool_chain"), sem("dve_chain"), sem("dve_places")
        ids_ready, ids_spread, onehot_ready = map(sem, ("ids_ready", "ids_spread", "onehot_ready"))
        cols_psum, cols_ready, qkvT_psum, qkvT_ready = map(sem, ("cols_psum", "cols_ready", "qkvT_psum", "qkvT_ready"))
        x0_psum, x0_used = sem("x0_psum"), sem("x0_used")
        ln_ready = [sem(f"ln{i}_ready") for i in range(LNS)]
        normed = [sem(f"normed{i}") for i in range(LNS)]
        xhatT_psum, x1T_ready, convg_psum, conva_psum = map(sem, ("xhatT_psum", "x1T_ready", "convg_psum", "conva_psum"))
        tanh_ready, a_ready, glu_ready, zT_ready, z_psum = map(sem, ("tanh_ready", "a_ready", "glu_ready", "zT_ready", "z_psum"))
        scaled_ready, h0_ready = sem("scaled_ready"), sem("h0_ready")
        xaT_psum, xaT_ready, qkv_psum, spikes_ready = map(sem, ("xaT_psum", "xaT_ready", "qkv_psum", "spikes_ready"))
        score_psum, routed_ready, attn_psum, h1_ready = map(sem, ("score_psum", "routed_ready", "attn_psum", "h1_ready"))
        xfT_psum, xfT_ready, logits_psum = map(sem, ("xfT_psum", "xfT_ready", "logits_psum"))
        shifted_ready, exp_ready, chosen_ready, rank_psum, slots_ready = map(
            sem, ("shifted_ready", "exp_ready", "chosen_ready", "rank_psum", "slots_ready"))
        count_psum, count_ready, table_ready = map(sem, ("count_psum", "count_ready", "table_ready"))
        rows_out, zeros_out, dummy_out = map(sem, ("rows_out", "zeros_out", "dummy_out"))
        xt_in = [sem(f"xt_in{i}") for i in range(U)]
        placed = [sem(f"placed{i}") for i in range(U)]
        t_xT_psum, t_xT, t_h_psum, t_h, t_act, t_actT_psum, t_actT, t_y_psum, t_y, t_place = map(
            sem, ("t_xT_psum", "t_xT", "t_h_psum", "t_h", "t_act", "t_actT_psum", "t_actT", "t_y_psum", "t_y", "t_place"))
        parts_in = [sem(f"parts_in{g}") for g in range(GROUPS)]
        base_ready, y_out, stored = sem("base_ready"), sem("y_out"), sem("stored")

        def blocks(ap, s):
            return ap[:, s * P:(s + 1) * P]

        def by_seq(ap, n=P):
            return ap.rearrange("p (s n) -> p s n", n=n)

        STAGES = ["x0", "ln0", "xhatT", "conv", "glu", "z", "ln1", "scale", "ln2", "xaT", "qkv",
                  "score", "attn", "ln3", "xfT", "logits", "route", "rank"]
        BEHIND = 4

        def front(program):
            for step in range(len(STAGES) + BEHIND * (GROUPS - 1)):
                for g in range(GROUPS):
                    at = step - BEHIND * g
                    if 0 <= at < len(STAGES) and STAGES[at] in program:
                        program[STAGES[at]](g)

        TILE_STEPS = dict(load_expert=0, turn_x=0, evacuate_x=0, places=0, first=1, add_b1=1, gelu=2, turn_act=3,
                          evacuate_act=3, second=4, add_b2=4)

        def experts(**program):
            for step in range(TILES + max(TILE_STEPS.values())):
                for name, run in program.items():
                    if 0 <= step - TILE_STEPS[name] < TILES:
                        run(step - TILE_STEPS[name])

        def experts_of(eng):
            of = {}

            def load_expert(j):
                if j < FULL:
                    e = eng.value_load(tile_w[0:1, j:j + 1], min_val=0, max_val=EXPERTS - 1)
                    of[j] = bass.ds(e, 1)
                else:
                    of[j] = slice(j - FULL, j - FULL + 1)
            return load_expert, of.__getitem__

        def flat(ap):
            return ap.rearrange("p o n -> p (o n)")

        work = dict(x0=work_a, xhat=work_b, tanh=work_c, a=work_d, glu=work_a, zT=work_b,
                    zhat=work_c, scaled=work_d, xa=work_a, xaT=work_b, xfT=work_c)

        def zero_fill(eng, e):
            n = eng.value_load(count_i[0:1, e:e + 1], min_val=0, max_val=T)
            eng.dma_start(slots[bass.ds(n + e * REGION, P), :], zero_rows[:]).then_inc(zeros_out, 16)

        block = ctx.enter_context(nc.Block())

        @block.sync
        def _(sp):
            sp.dma_start(ids_i[:], x).then_inc(ids_in, 16)
            sp.dma_start(emb_sb[:], emb).then_inc(emb_in, 16)
            sp.dma_start(pos_sb[:], pos).then_inc(emb_in, 16)
            for i, row in enumerate((g1, b1, conv_b[0:D], conv_b[D:2 * D])):
                sp.dma_start(rows4[i:i + 1, :], row.rearrange("(o n) -> o n", o=1)).then_inc(rows_in, 16)
            sp.dma_start(convw_sb[:], conv_w.rearrange("w i o -> i w o")).then_inc(conv_in, 16)
            for i, w in enumerate((Wq, Wk, Wv)):
                sp.dma_start(wqkv[:, i, :], w).then_inc(qkv_in, 16)
            sp.dma_start(g2_bc[:], g2.partition_broadcast(P)).then_inc(gb2_in, 16)
            sp.dma_start(b2_bc[:], b2.partition_broadcast(P)).then_inc(gb2_in, 16)
            sp.dma_start(wr_sb[:], Wr).then_inc(router_in, 16)
            sp.dma_start(br_bc[:], br.partition_broadcast(P)).then_inc(router_in, 16)
            sp.dma_start(w1_sb[:], W1.rearrange("e d h -> d e h")).then_inc(w1_in, 16)
            sp.dma_start(w2_sb[:], W2.rearrange("e (c p) d -> p e c d", p=P)).then_inc(w2_in, 16)
            sp.dma_start(fb1_bc[:].rearrange("p e h -> p (e h)"),
                         fb1.rearrange("e h -> (e h)").partition_broadcast(P)).then_inc(fb_in, 16)
            sp.dma_start(fb2_bc[:].rearrange("p e d -> p (e d)"),
                         fb2.rearrange("e d -> (e d)").partition_broadcast(P)).then_inc(fb_in, 16)
            sp.wait_ge(consts_ready, 1)
            sp.dma_start(slots[DUMMY:DUMMY + P, :], zero_rows[:]).then_inc(dummy_out, 16)

            sp.wait_ge(count_ready, 1)
            for e in range(EXPERTS // 2):
                zero_fill(sp, e)

            sp.wait_ge(table_ready, 1)
            sp.wait_ge(dummy_out, 16)
            sp.wait_ge(rows_out, 16 * TOPK * SEQS)
            for j in range(TILES):
                u = j % U
                if j < FULL:
                    row = sp.value_load(tile_row[0:1, j:j + 1], min_val=0, max_val=DUMMY)
                else:
                    row = sp.value_load(tail_row[0:1, j - FULL:j - FULL + 1], min_val=0, max_val=DUMMY - P)
                if j == FULL:
                    sp.wait_ge(zeros_out, 16 * EXPERTS)
                if j >= U:
                    sp.wait_ge(t_xT_psum, j - U + 1)
                    sp.wait_ge(t_place, j - U + 1)
                sp.dma_start(xt[:, u, :], slots[bass.ds(row, P), :]).then_inc(xt_in[u], 16)

            for u in range(U):
                sp.wait_ge(placed[u], 16 * (TILES // U))
            both = parts.rearrange("(k b p) d -> k p b d", k=TOPK, p=P)
            for g in range(GROUPS):
                for k, buf in enumerate((work_a, work_b)):
                    sp.dma_start(by_seq(buf[:, g, :]), both[k, :, g * GS:(g + 1) * GS, :]).then_inc(parts_in[g], 16)
            tokens = out.rearrange("b t d -> t b d")
            for g in range(GROUPS):
                sp.wait_ge(y_out, g + 1)
                sp.dma_start(tokens[:, g * GS:(g + 1) * GS, :], by_seq(work_c[:, g, :])).then_inc(stored, 16)
            sp.wait_ge(stored, 16 * GROUPS)

        @block.gpsimd
        def _(pool):
            done = [0]

            def link(ins):
                done[0] += 1
                ins.then_inc(pool_chain, 1)
                pool.wait_ge(pool_chain, done[0])

            pool.memset(ident[:], 0.0)
            pool.memset(ones_b[:], 1.0)
            pool.memset(zero_rows[:], 0.0)
            pool.memset(zeros_e[:], 0.0)
            pool.memset(causal[:], 1.0)
            pool.memset(stage[:], 0.0)
            pool.memset(chosen_sum[:, 0, :], 0.0)
            link(pool.memset(x1T[:], 0.0))
            link(pool.affine_select(out=ident[:], in_=ident[:], compare_op=ALU.not_equal, fill=1.0, base=0,
                                    pattern=[[-1, P]], channel_multiplier=1))
            pool.affine_select(out=causal[:], in_=causal[:], compare_op=ALU.is_ge, fill=0.0, base=0,
                               pattern=[[1, P]], channel_multiplier=-1)
            pool.affine_select(out=before_b[:], in_=ones_b[:], compare_op=ALU.is_gt, fill=0.0, base=0,
                               pattern=[[1, P]], channel_multiplier=-1)
            pool.iota(part_id[:], pattern=[[0, 1]], base=0, channel_multiplier=1, allow_small_or_imprecise_dtypes=True)
            pool.iota(expert_id[:], pattern=[[1, EXPERTS]], base=0, channel_multiplier=0,
                      allow_small_or_imprecise_dtypes=True)
            pool.iota(region_at[:], pattern=[[REGION, EXPERTS]], base=0, channel_multiplier=0,
                      allow_small_or_imprecise_dtypes=True)
            pool.iota(tile_id[:], pattern=[[1, FULL]], base=0, channel_multiplier=0,
                      allow_small_or_imprecise_dtypes=True)
            pool.iota(stage[:, :, :, ROW_PLACE:ROW_PLACE + 1], pattern=[[N, GROUPS], [P, GS], [0, 1]], base=T,
                      channel_multiplier=1, allow_small_or_imprecise_dtypes=True)
            pool.memset(zero_rows[:, ROW_PLACE:ROW_PLACE + 1], NOWHERE)
            pool.tensor_copy(ident_b[:], ident[:]).then_inc(consts_ready, 1)

            def add_x1(g):
                pool.wait_ge(glu_ready, g + 1)
                pool.tensor_tensor(by_seq(work["zT"][:, g, :]), by_seq(work["glu"][:, g, :]),
                                   x1T[:, g, :, PAD:], ALU.add).then_inc(zT_ready, 1)

            def scale_g2(g):
                if g == 0:
                    pool.wait_ge(gb2_in, 32)
                pool.wait_ge(normed[1], g + 1)
                pool.tensor_tensor(by_seq(work["scaled"][:, g, :]), by_seq(work["zhat"][:, g, :]),
                                   g2_bc[:].unsqueeze(1).broadcast_to([P, GS, D]), ALU.mult).then_inc(scaled_ready, 1)

            def scatter_rows(g):
                pool.wait_ge(slots_ready, g + 1)
                for s in range(GS):
                    for k in range(TOPK):
                        pool.indirect_dma_start(
                            out=slots, out_offset=bass.IndirectOffsetOnAxis(
                                ap=slot_of[:, g, k, s:s + 1].bitcast(U32), axis=0),
                            in_=stage[:, g, s, :], in_offset=None).then_inc(rows_out, 16)

            front(dict(glu=add_x1, scale=scale_g2, rank=scatter_rows))

            last_place = pool.to_reg(TOPK * T - 1)

            for j in range(TILES):
                u = j % U
                pool.wait_ge(t_y, j + 1)
                pool.wait_ge(t_place, j + 1)
                pool.indirect_dma_start(
                    out=parts, out_offset=bass.IndirectOffsetOnAxis(ap=place[:, u:u + 1].bitcast(U32), axis=0),
                    in_=y_sb[:, u, :], in_offset=None, bounds_check=last_place,
                    oob_is_err=False).then_inc(placed[u], 16)

        @block.scalar
        def _(act):
            act.wait_ge(cols_psum, 1)
            act.activation(cols4[:, 0:2], bank[7][:, 0:2], ACT.Copy)
            act.activation(cols4[:, 2:4], bank[7][:, 2:4], ACT.Copy, scale=0.5).then_inc(cols_ready, 1)
            act.wait_ge(qkvT_psum, 1)
            act.activation(wqkvT[:].rearrange("p w n -> p (w n)"), bank[6][:, 0:3 * D], ACT.Copy).then_inc(qkvT_ready, 1)
            act.wait_ge(cols_ready, 1)

            def normalise(g, which, src, dst):
                act.wait_ge(ln_ready[which], g + 1)
                for s in range(GS):
                    last = act.activation(dst[s], src[s], ACT.Identity, scale=rs_work[:, which, g, 8, s:s + 1],
                                          bias=rs_work[:, which, g, 9, s:s + 1])
                last.then_inc(normed[which], 1)

            def parts_of(buf, g):
                return [blocks(buf[:, g, :], s) for s in range(GS)]

            def norm_x0(g):
                normalise(g, 0, parts_of(work["x0"], g), parts_of(work["xhat"], g))

            def evacuate_x1T(g):
                act.wait_ge(xhatT_psum, g + 1)
                act.activation(x1T[:, g, :, PAD:], by_seq(bank[0][:]), ACT.Identity, scale=cols4[:, 0:1],
                               bias=cols4[:, 1:2]).then_inc(x1T_ready, 1)

            def gate(g):
                act.wait_ge(convg_psum, g + 1)
                act.activation(work["tanh"][:, g, :], bank[2][:], ACT.Tanh, scale=0.5,
                               bias=cols4[:, 3:4]).then_inc(tanh_ready, 1)
                act.wait_ge(conva_psum, g + 1)
                act.activation(work["a"][:, g, :], bank[3][:], ACT.Identity, scale=0.5,
                               bias=cols4[:, 2:3]).then_inc(a_ready, 1)

            def norm_z(g):
                normalise(g, 1, [blocks(bank[1], s) for s in range(GS)], parts_of(work["zhat"], g))

            def norm_h0(g):
                normalise(g, 2, parts_of(h0, g), parts_of(work["xa"], g))

            def evacuate_xaT(g):
                act.wait_ge(xaT_psum, g + 1)
                act.activation(work["xaT"][:, g, :], bank[1][:], ACT.Copy).then_inc(xaT_ready, 1)

            def norm_h1(g):
                normalise(g, 3, parts_of(h1, g), [stage[:, g, s, 0:D] for s in range(GS)])

            def evacuate_xfT(g):
                act.wait_ge(xfT_psum, g + 1)
                act.activation(work["xfT"][:, g, :], bank[6][:], ACT.Copy).then_inc(xfT_ready, 1)

            def exp_logits(g):
                act.wait_ge(shifted_ready, g + 1)
                act.activation(probs[:, g, 2, :], probs[:, g, 1, :], ACT.Exp).then_inc(exp_ready, 1)

            front(dict(ln0=norm_x0, xhatT=evacuate_x1T, conv=gate, ln1=norm_z, ln2=norm_h0, xaT=evacuate_xaT,
                       ln3=norm_h1, xfT=evacuate_xfT, route=exp_logits))

            act.wait_ge(count_ready, 1)
            for e in range(EXPERTS // 2, EXPERTS):
                zero_fill(act, e)

            def evacuate_x(j):
                b = j % 2
                act.wait_ge(t_xT_psum, j + 1)
                if j >= 2:
                    act.wait_ge(t_h_psum, j - 1)
                act.activation(xtT[:, b, :], bank[b][:, 0:P], ACT.Copy).then_inc(t_xT, 1)

            def gelu(j):
                b = j % 2
                act.wait_ge(t_h, j + 1)
                if j >= 2:
                    act.wait_ge(t_actT_psum, j - 1)
                act.activation(act_h[:, b, :], hid[:, b, :], ACT.Gelu).then_inc(t_act, 1)

            def evacuate_act(j):
                b = j % 2
                act.wait_ge(t_actT_psum, j + 1)
                if j >= 2:
                    act.wait_ge(t_y_psum, j - 1)
                act.activation(act_hT[:, b, :], bank[4 + b][:, 0:HID], ACT.Copy).then_inc(t_actT, 1)

            experts(evacuate_x=evacuate_x, evacuate_act=evacuate_act, gelu=gelu)

        @block.vector
        def _(dve):
            done = [0]

            def link(ins):
                done[0] += 1
                ins.then_inc(dve_chain, 1)
                dve.wait_ge(dve_chain, done[0])

            dve.wait_ge(ids_in, 16)
            link(dve.tensor_scalar(ids_f[:, 0, :], ids_i[:], 0.0, float(ROWS_EMB), ALU.is_lt, ALU.mult))
            link(dve.tensor_tensor(ids_f[:, 1, :], ids_f[:, 0, :], ids_i[:], ALU.add))
            dve.tensor_scalar(ids_b[:], ids_f[:, 1, :], 0.0, float(ROWS_EMB - 1), ALU.max,
                              ALU.min).then_inc(ids_ready, 1)
            dve.wait_ge(consts_ready, 1)
            for g in range(GROUPS):
                dve.wait_ge(ids_spread, g + 1)
                dve.tensor_scalar(onehot[:, g, :], bank[2 + g][0:ROWS_EMB, :], part_id[0:ROWS_EMB, :], None,
                                  ALU.is_equal).then_inc(onehot_ready, 1)

            def rsqrt(g, which):
                w = [rs_work[:, which, g, i, :] for i in range(10)]
                var, mean = mean_var[:, which, g, :, 1], mean_var[:, which, g, :, 0]
                v, y, y2, h, q, z, z2, c = w[:8]
                link(dve.tensor_scalar(v, var, LN_EPS, None, ALU.add))
                link(dve.tensor_scalar(y.bitcast(I32), v.bitcast(I32), -0.5, RSQRT_SEED, ALU.mult, ALU.add))
                link(dve.tensor_tensor(y2, y, y, ALU.mult))
                link(dve.tensor_tensor(h, y2, v, ALU.mult))
                link(dve.scalar_tensor_tensor(out=q, in0=h, scalar=-10 / 3, in1=h, op0=ALU.add, op1=ALU.mult))
                link(dve.scalar_tensor_tensor(out=z, in0=q, scalar=5.0, in1=y, op0=ALU.add, op1=ALU.mult))
                link(dve.tensor_tensor(z2, z, z, ALU.mult))
                link(dve.tensor_tensor(y2, z2, v, ALU.mult))
                link(dve.tensor_scalar(c, y2, -0.5 * 0.375 ** 3, 1.5 * 0.375, ALU.mult, ALU.add))
                link(dve.tensor_tensor(w[8], z, c, ALU.mult))
                dve.scalar_tensor_tensor(out=w[9], in0=mean, scalar=-1.0, in1=w[8], op0=ALU.mult,
                                         op1=ALU.mult).then_inc(ln_ready[which], 1)

            def layer_stats(g, which, src):
                for s in range(GS):
                    last = dve.bn_stats(stats[:, which, g, s, :], blocks(src, s))
                link(last)
                for s in range(GS):
                    last = dve.bn_aggr(mean_var[:, which, g, s, :], stats[:, which, g, s, :])
                link(last)
                rsqrt(g, which)

            def add_pos(g):
                if g == 0:
                    dve.wait_ge(emb_in, 32)
                dve.wait_ge(x0_psum, g + 1)
                x0 = work["x0"][:, g, :]
                link(dve.tensor_tensor(by_seq(x0), by_seq(bank[0][:]), pos_sb[:].unsqueeze(1).broadcast_to([P, GS, D]),
                                       ALU.add))
                layer_stats(g, 0, x0)

            def glu(g):
                dve.wait_ge(tanh_ready, g + 1)
                dve.wait_ge(a_ready, g + 1)
                dve.scalar_tensor_tensor(out=work["glu"][:, g, :], in0=work["tanh"][:, g, :], scalar=1.0,
                                         in1=work["a"][:, g, :], op0=ALU.add, op1=ALU.mult).then_inc(glu_ready, 1)

            def stats_z(g):
                dve.wait_ge(z_psum, g + 1)
                layer_stats(g, 1, bank[1])

            def add_b2(g):
                dve.wait_ge(scaled_ready, g + 1)
                link(dve.tensor_tensor(by_seq(h0[:, g, :]), by_seq(work["scaled"][:, g, :]),
                                       b2_bc[:].unsqueeze(1).broadcast_to([P, GS, D]), ALU.add))
                layer_stats(g, 2, h0[:, g, :])

            def spikes(g):
                dve.wait_ge(qkv_psum, g + 1)
                dve.tensor_scalar(spike_q[:, g, :], bank[4][:], Q_THRESH, None, ALU.is_ge)
                dve.tensor_scalar(spike_k[:, g, :], bank[5][:], K_THRESH, None, ALU.is_ge)
                dve.tensor_scalar(spike_v[:, g, :], bank[6][:], V_THRESH, None, ALU.is_ge).then_inc(spikes_ready, 1)

            def route_mask(g):
                dve.wait_ge(score_psum, g + 1)
                dve.scalar_tensor_tensor(out=by_seq(routed[:, g, :]), in0=by_seq(bank[5][:]), scalar=MASK_THRESH,
                                         in1=causal[:].unsqueeze(1).broadcast_to([P, GS, P]), op0=ALU.is_gt,
                                         op1=ALU.mult).then_inc(routed_ready, 1)

            def add_attn(g):
                dve.wait_ge(attn_psum, g + 1)
                link(dve.tensor_tensor(h1[:, g, :], bank[4][:], h0[:, g, :], ALU.add))
                layer_stats(g, 3, h1[:, g, :])

            def by_expert(ap):
                return ap.rearrange("p (s e) -> p s e", e=EXPERTS)

            def over_experts(ap):
                return ap.unsqueeze(2).broadcast_to([P, GS, EXPERTS])

            def shift_logits(g):
                if g == 0:
                    dve.wait_ge(router_in, 32)
                dve.wait_ge(logits_psum, g + 1)
                logits, shifted = by_expert(probs[:, g, 0, :]), by_expert(probs[:, g, 1, :])
                link(dve.tensor_tensor(logits, by_expert(bank[7][:, 0:GS * EXPERTS]),
                                       br_bc[:].unsqueeze(1).broadcast_to([P, GS, EXPERTS]), ALU.add))
                link(dve.tensor_reduce(row_stat[:, g, 0, :], logits, AX_X, ALU.max))
                dve.tensor_tensor(shifted, logits, over_experts(row_stat[:, g, 0, :]),
                                  ALU.subtract).then_inc(shifted_ready, 1)

            def choose(g):
                dve.wait_ge(exp_ready, g + 1)
                e, p = by_expert(probs[:, g, 2, :]), by_expert(probs[:, g, 3, :])
                link(dve.tensor_reduce(row_stat[:, g, 1, :], e, AX_X, ALU.add))
                link(dve.reciprocal(row_stat[:, g, 2, :], row_stat[:, g, 1, :]))
                link(dve.tensor_tensor(p, e, over_experts(row_stat[:, g, 2, :]), ALU.mult))
                for s in range(GS):
                    last = dve.max(top8[:, g, s, :], p[:, s, :])
                link(last)
                for s in range(GS):
                    last = dve.max_index(top8_at[:, g, s, :], top8[:, g, s, :], p[:, s, :])
                link(last)
                link(dve.tensor_copy(top_at[:, g, :, :], top8_at[:, g, :, 0:TOPK]))
                for k in range(TOPK):
                    last = dve.tensor_tensor(by_expert(chosen[:, g, k, :]),
                                             expert_id[:].unsqueeze(1).broadcast_to([P, GS, EXPERTS]),
                                             over_experts(top_at[:, g, :, k]), ALU.is_equal)
                link(last)
                dve.tensor_tensor(chosen_b[:, g, :], chosen[:, g, 0, :], chosen[:, g, 1, :],
                                  ALU.add).then_inc(chosen_ready, 1)
                link(dve.tensor_tensor(w_work[:, g, 0, :], top8[:, g, :, 0], top8[:, g, :, 1], ALU.add))
                link(dve.tensor_scalar(w_work[:, g, 1, :], w_work[:, g, 0, :], TOPK_FLOOR, None, ALU.max))
                link(dve.reciprocal(w_work[:, g, 2, :], w_work[:, g, 1, :]))
                for k in range(TOPK):
                    dve.tensor_tensor(w_top[:, g, k, :], top8[:, g, :, k], w_work[:, g, 2, :], ALU.mult)
                counts = chosen_b[:, g, :].rearrange("p (s e) -> p e s", e=EXPERTS)
                link(dve.tensor_reduce(rank_at[:, g, 2, 0:EXPERTS], counts, AX_X, ALU.add))
                dve.tensor_tensor(chosen_sum[:, g + 1, :], rank_at[:, g, 2, 0:EXPERTS], chosen_sum[:, g, :],
                                  ALU.add).then_inc(chosen_ready, 1)

            def slots_of(g):
                dve.wait_ge(rank_psum, g + 1)
                at = by_expert(rank_at[:, g, 0, :])
                link(dve.tensor_tensor(at, by_expert(bank[7][:, 64:64 + GS * EXPERTS]),
                                       region_at[:].unsqueeze(1).broadcast_to([P, GS, EXPERTS]), ALU.add))
                link(dve.tensor_tensor(rank_at[:, g, 1:3, :], chosen[:, g, :, :],
                                       rank_at[:, g, 0:1, :].broadcast_to([P, TOPK, GS * EXPERTS]), ALU.mult))
                link(dve.tensor_reduce(slot_f[:, g, :], rank_at[:, g, 1:3, :].rearrange("p k (s e) -> p (k s) e", e=EXPERTS),
                                       AX_X, ALU.add))
                dve.tensor_copy(slot_of[:, g, :, :].rearrange("p k s -> p (k s)"), slot_f[:, g, :])
                dve.wait_ge(normed[3], g + 1)
                dve.tensor_copy(stage[:, g, :, ROW_FIRST], top_at[:, g, :, 0]).then_inc(slots_ready, 1)

            front(dict(x0=add_pos, glu=glu, z=stats_z, scale=add_b2, qkv=spikes, score=route_mask, attn=add_attn,
                       logits=shift_logits, route=choose, rank=slots_of))

            dve.wait_ge(count_psum, 1)
            dve.tensor_copy(count_i[:], bank[7][:, 128:128 + EXPERTS]).then_inc(count_ready, 1)
            dve.wait_ge(count_ready, 1)
            link(dve.tensor_scalar(tiles_i[:], count_i[:], P.bit_length() - 1, None, ALU.logical_shift_right))
            link(dve.tensor_copy(tiles_f[:], tiles_i[:]))
            dve.tensor_scalar(skip_rows[:], tiles_f[:], -float(P), float(REGION), ALU.mult, ALU.add)
            dve.scalar_tensor_tensor(out=tail_row[:], in0=tiles_f[:], scalar=float(P), in1=region_at[:], op0=ALU.mult,
                                     op1=ALU.add)
            link(dve.tensor_tensor_scan(tiles_upto[:], tiles_f[:], zeros_e[:], 0.0, ALU.add, ALU.add))
            every = [P, FULL, EXPERTS]
            link(dve.tensor_tensor(done_before[:], tile_id[:].unsqueeze(2).broadcast_to(every),
                                   tiles_upto[:].unsqueeze(1).broadcast_to(every), ALU.is_ge))
            dve.tensor_tensor(skipped[:], done_before[:], skip_rows[:].unsqueeze(1).broadcast_to(every), ALU.mult)
            link(dve.tensor_reduce(tile_expert[:], done_before[:], AX_X, ALU.add))
            link(dve.tensor_reduce(tile_skip[:], skipped[:], AX_X, ALU.add))
            dve.tensor_scalar(tile_w[:], tile_expert[:], float(EXPERTS - 1), None, ALU.min)
            link(dve.scalar_tensor_tensor(out=tile_row_f[:], in0=tile_id[:], scalar=float(P), in1=tile_skip[:],
                                          op0=ALU.mult, op1=ALU.add))
            dve.tensor_scalar(tile_row[:], tile_row_f[:], float(DUMMY), None, ALU.min).then_inc(table_ready, 1)

            for g in range(GROUPS):
                last = dve.tensor_tensor(by_seq(h0[:, g, :]), by_seq(h1[:, g, :]), stage[:, g, :, 0:D], ALU.add)
            last.then_inc(base_ready, 1)

            dve.wait_ge(table_ready, 1)
            dve.wait_ge(fb_in, 32)

            load_expert, expert_of = experts_of(dve)

            def add_b1(j):
                b = j % 2
                dve.wait_ge(t_h_psum, j + 1)
                if j >= 2:
                    dve.wait_ge(t_act, j - 1)
                dve.tensor_tensor(hid[:, b, :], bank[2 + b][:, 0:HID], flat(fb1_bc[:, expert_of(j), :]),
                                  ALU.add).then_inc(t_h, 1)

            def places(j):
                u = j % U
                dve.wait_ge(xt_in[u], 16 * (j // U + 1))
                if j >= U:
                    dve.wait_ge(placed[u], 16 * (j // U))
                expert = tile_expert[:, j:j + 1] if j < FULL else float(j - FULL)
                dve.tensor_scalar(other[:, u:u + 1], xt[:, u, ROW_FIRST:ROW_FIRST + 1], expert, -float(T),
                                  ALU.is_equal, ALU.mult).then_inc(dve_places, 1)
                dve.wait_ge(dve_places, j + 1)
                dve.tensor_tensor(place[:, u:u + 1], other[:, u:u + 1], xt[:, u, ROW_PLACE:ROW_PLACE + 1],
                                  ALU.add).then_inc(t_place, 1)

            def add_b2(j):
                u, b = j % U, j % 2
                dve.wait_ge(t_y_psum, j + 1)
                if j >= U:
                    dve.wait_ge(placed[u], 16 * (j // U))
                dve.tensor_tensor(y_sb[:, u, :], bank[6 + b][:, 0:D], flat(fb2_bc[:, expert_of(j), :]),
                                  ALU.add).then_inc(t_y, 1)

            experts(load_expert=load_expert, add_b1=add_b1, places=places, add_b2=add_b2)

            for g in range(GROUPS):
                dve.wait_ge(parts_in[g], 32)
                for s in range(GS):
                    link_last = dve.scalar_tensor_tensor(
                        out=blocks(work_d[:, g, :], s), in0=blocks(work_a[:, g, :], s), scalar=w_top[:, g, 0, s:s + 1],
                        in1=blocks(h0[:, g, :], s), op0=ALU.mult, op1=ALU.add)
                link(link_last)
                for s in range(GS):
                    last = dve.scalar_tensor_tensor(
                        out=blocks(work_c[:, g, :], s), in0=blocks(work_b[:, g, :], s), scalar=w_top[:, g, 1, s:s + 1],
                        in1=blocks(work_d[:, g, :], s), op0=ALU.mult, op1=ALU.add)
                last.then_inc(y_out, 1)

        @block.tensor
        def _(pe):
            pe.wait_ge(consts_ready, 1)
            pe.wait_ge(ids_ready, 1)
            for g in range(GROUPS):
                for s in range(GS):
                    b = g * GS + s
                    last = pe.matmul(blocks(bank[2 + g][0:ROWS_EMB, :], s),
                                     ident_b[0:SEQS, b:b + 1].broadcast_to([SEQS, ROWS_EMB]), ids_b[:],
                                     start=True, stop=True)
                last.then_inc(ids_spread, 1)
            pe.wait_ge(rows_in, 64)
            pe.transpose(bank[7][:, 0:4], rows4[:], ident[0:4, 0:4]).then_inc(cols_psum, 1)
            pe.wait_ge(qkv_in, 48)
            pe.wait_ge(onehot_ready, GROUPS)
            for i in range(3):
                last = pe.transpose(bank[6][:, i * D:(i + 1) * D], wqkv[:, i, :], ident[:])
            last.then_inc(qkvT_psum, 1)

            def turn(dst, src):
                for s in range(GS):
                    last = pe.transpose(blocks(dst, s), src[s], ident[:])
                return last

            def parts_of(buf, g):
                return [blocks(buf[:, g, :], s) for s in range(GS)]

            def lookup(g):
                if g == 0:
                    pe.wait_ge(emb_in, 32)
                pe.wait_ge(onehot_ready, g + 1)
                if g >= 1:
                    pe.wait_ge(x1T_ready, g)
                for s in range(GS):
                    last = pe.matmul(blocks(bank[0], s), blocks(onehot[:, g, :], s), emb_sb[:], start=True, stop=True)
                last.then_inc(x0_psum, 1)

            def turn_xhat(g):
                pe.wait_ge(normed[0], g + 1)
                turn(bank[0], parts_of(work["xhat"], g)).then_inc(xhatT_psum, 1)

            def conv(g):
                if g == 0:
                    pe.wait_ge(conv_in, 16)
                pe.wait_ge(x1T_ready, g + 1)
                for half, acc, free, full in ((1, bank[2], tanh_ready, convg_psum), (0, bank[3], a_ready, conva_psum)):
                    if g >= 1:
                        pe.wait_ge(free, g)
                    for w in range(TAPS):
                        last = pe.matmul(by_seq(acc[:]), convw_sb[:, w, half * D:(half + 1) * D],
                                         x1T[:, g, :, w:w + L], start=(w == 0), stop=(w == TAPS - 1))
                    last.then_inc(full, 1)

            def turn_z(g):
                pe.wait_ge(zT_ready, g + 1)
                if g >= 1:
                    pe.wait_ge(xaT_ready, g)
                turn(bank[1], parts_of(work["zT"], g)).then_inc(z_psum, 1)

            def turn_xa(g):
                pe.wait_ge(normed[2], g + 1)
                turn(bank[1], parts_of(work["xa"], g)).then_inc(xaT_psum, 1)

            def project(g):
                if g == 0:
                    pe.wait_ge(qkvT_ready, 1)
                pe.wait_ge(xaT_ready, g + 1)
                if g >= 1:
                    pe.wait_ge(ln_ready[3], g)
                    pe.wait_ge(xfT_ready, g)
                xaT = work["xaT"][:, g, :]
                pe.matmul(bank[4][:], wqkvT[:, 0, :], xaT, start=True, stop=True)
                pe.matmul(bank[5][:], wqkvT[:, 1, :], xaT, start=True, stop=True)
                for s in range(GS):
                    last = pe.matmul(blocks(bank[6], s), blocks(xaT, s), wqkvT[:, 2, :], start=True, stop=True)
                last.then_inc(qkv_psum, 1)

            def score(g):
                pe.wait_ge(spikes_ready, g + 1)
                for s in range(GS):
                    last = pe.matmul(blocks(bank[5], s), blocks(spike_k[:, g, :], s), blocks(spike_q[:, g, :], s),
                                     start=True, stop=True)
                last.then_inc(score_psum, 1)

            def attend(g):
                pe.wait_ge(routed_ready, g + 1)
                for s in range(GS):
                    last = pe.matmul(blocks(bank[4], s), blocks(routed[:, g, :], s), blocks(spike_v[:, g, :], s),
                                     start=True, stop=True)
                last.then_inc(attn_psum, 1)

            def turn_xf(g):
                pe.wait_ge(normed[3], g + 1)
                turn(bank[6], [stage[:, g, s, 0:D] for s in range(GS)]).then_inc(xfT_psum, 1)

            def router(g):
                if g == 0:
                    pe.wait_ge(router_in, 32)
                pe.wait_ge(xfT_ready, g + 1)
                if g >= 1:
                    pe.wait_ge(slots_ready, g)
                for s in range(GS):
                    last = pe.matmul(bank[7][:, s * EXPERTS:(s + 1) * EXPERTS], blocks(work["xfT"][:, g, :], s),
                                     wr_sb[:], start=True, stop=True)
                last.then_inc(logits_psum, 1)

            def rank(g):
                pe.wait_ge(chosen_ready, 2 * g + 2)
                ranks = bank[7][:, 64:64 + GS * EXPERTS]
                pe.matmul(ranks, before_b[:], chosen_b[:, g, :], start=True, stop=False)
                for s in range(GS - 1):
                    behind = GS - 1 - s
                    pe.matmul(ranks[:, (s + 1) * EXPERTS:].rearrange("p (s e) -> p s e", e=EXPERTS), ones_b[:],
                              chosen_b[:, g, s * EXPERTS:(s + 1) * EXPERTS].unsqueeze(1)
                              .broadcast_to([P, behind, EXPERTS]), start=False, stop=False)
                pe.matmul(ranks.rearrange("p (s e) -> p s e", e=EXPERTS), ones_b[:],
                          chosen_sum[:, g, :].unsqueeze(1).broadcast_to([P, GS, EXPERTS]),
                          start=False, stop=True).then_inc(rank_psum, 1)
                if g == GROUPS - 1:
                    pe.wait_ge(slots_ready, GROUPS)
                    pe.matmul(bank[7][:, 128:128 + EXPERTS], ones_b[:], chosen_sum[:, GROUPS, :],
                              start=True, stop=True).then_inc(count_psum, 1)

            front(dict(x0=lookup, xhatT=turn_xhat, conv=conv, z=turn_z, xaT=turn_xa, qkv=project, score=score,
                       attn=attend, xfT=turn_xf, logits=router, rank=rank))

            pe.wait_ge(table_ready, 1)
            pe.wait_ge(w1_in, 16)
            pe.wait_ge(w2_in, 16)

            load_expert, expert_of = experts_of(pe)

            def turn_x(j):
                u, b = j % U, j % 2
                pe.wait_ge(xt_in[u], 16 * (j // U + 1))
                if j >= 2:
                    pe.wait_ge(t_xT, j - 1)
                pe.transpose(bank[b][:, 0:P], xt[:, u, 0:D], ident[:]).then_inc(t_xT_psum, 1)

            def first(j):
                b = j % 2
                pe.wait_ge(t_xT, j + 1)
                if j >= 2:
                    pe.wait_ge(t_h, j - 1)
                pe.matmul(bank[2 + b][:, 0:HID], xtT[:, b, :], flat(w1_sb[:, expert_of(j), :]),
                          start=True, stop=True).then_inc(t_h_psum, 1)

            def turn_act(j):
                b = j % 2
                pe.wait_ge(t_act, j + 1)
                if j >= 2:
                    pe.wait_ge(t_actT, j - 1)
                for c in range(2):
                    last = pe.transpose(bank[4 + b][:, c * P:(c + 1) * P], act_h[:, b, c * P:(c + 1) * P], ident[:])
                last.then_inc(t_actT_psum, 1)

            def second(j):
                b = j % 2
                pe.wait_ge(t_actT, j + 1)
                if j >= 2:
                    pe.wait_ge(t_y, j - 1)
                for c in range(2):
                    last = pe.matmul(bank[6 + b][:, 0:D], act_hT[:, b, c * P:(c + 1) * P],
                                     flat(w2_sb[:, expert_of(j), c, :]), start=(c == 0), stop=(c == 1))
                last.then_inc(t_y_psum, 1)

            experts(load_expert=load_expert, turn_x=turn_x, turn_act=turn_act, second=second, first=first)


_INS = ["x", "fside_BS_emb", "L0_tok_pos", "L0_tok_g1", "L0_tok_b1", "L0_tok_conv_w", "L0_tok_conv_b", "L0_tok_g2",
        "L0_tok_b2", "L0_attn_Wq", "L0_attn_Wk", "L0_attn_Wv", "L0_ffn_Wr", "L0_ffn_br", "L0_ffn_W1", "L0_ffn_b1",
        "L0_ffn_W2", "L0_ffn_b2"]


def kernel(**inputs):
    import numpy as _np
    import concourse.bacc as _bacc
    from concourse import mybir as _mybir
    from concourse.bass_utils import run_bass_kernel_spmd as _run

    nc = _bacc.Bacc("TRN2", target_bir_lowering=False, num_devices=1)
    arrays, args = {}, []
    for name in _INS:
        a = _np.ascontiguousarray(inputs[name])
        arrays[f"in_{name}_dram"] = a
        args.append(nc.dram_tensor(f"in_{name}_dram", a.shape, _mybir.dt.from_np(a.dtype), kind="ExternalInput").ap())
    args.append(nc.dram_tensor("out_0_dram", (16, 128, 128), _mybir.dt.float32, kind="ExternalOutput").ap())
    tower_kernel(nc, *args)
    r = _run(nc, [arrays], core_ids=[0])
    return r.results[0]["out_0_dram"]
```

```python
from contextlib import ExitStack

import concourse.bass as bass
from concourse import mybir

F32 = mybir.dt.float32
BF16 = mybir.dt.bfloat16
I32 = mybir.dt.int32
U32 = mybir.dt.uint32
ALU = mybir.AluOpType
ACT = mybir.ActivationFunctionType
AX_X = mybir.AxisListType.X

P = 128
LN_EPS = 1e-5
Q_THRESH = K_THRESH = 0.25
V_THRESH = 0.3
MASK_THRESH = 0.1
TOPK_FLOOR = 1e-9
TOPK = 2
RSQRT_SEED = float(0x5F3759DF)
ROW = 132
ROW_PLACE = 128


def tower_kernel(nc, x, emb, pos, g1, b1, conv_w, conv_b, g2, b2, Wq, Wk, Wv, Wr, br, W1, fb1, W2, fb2, out):
    SEQS, L = x.shape
    ROWS_EMB, D = emb.shape
    TAPS = conv_w.shape[0]
    EXPERTS, _, HID = W1.shape
    assert L == P and D == P and HID == 2 * P
    T = SEQS * L
    GS = 4
    GROUPS = SEQS // GS
    N = GS * L
    PAD = TAPS - 1
    REGION = T + P
    DUMMY = EXPERTS * REGION
    SLOTS = DUMMY + P
    FULL = TOPK * T // P
    TILES = FULL + EXPERTS
    U = 16
    assert TILES % U == 0
    NOWHERE = 1 << 20

    slots = nc.dram_tensor("slots", [SLOTS, ROW], F32).ap()
    parts = nc.dram_tensor("parts", [TOPK * T, D], F32).ap()

    with ExitStack() as ctx:
        def sb(name, shape, dt=F32):
            return ctx.enter_context(nc.sbuf_tensor(name, shape, dt))

        def sem(name):
            return ctx.enter_context(nc.semaphore(name))

        bank = [ctx.enter_context(nc.psum_tensor(f"bank{i}", [P, 512], F32)) for i in range(8)]

        ids_i = sb("ids_i", [SEQS, L], I32)
        ids_f = sb("ids_f", [SEQS, 4, L])
        ids_b = sb("ids_b", [SEQS, L], BF16)
        emb_sb = sb("emb_sb", [ROWS_EMB, D])
        pos_sb = sb("pos_sb", [P, D])
        rows4 = sb("rows4", [4, P])
        cols4 = sb("cols4", [P, 4])
        convw_sb = sb("convw_sb", [P, TAPS, 2 * D])
        wqkv = sb("wqkv", [P, 3, D])
        wqkvT = sb("wqkvT", [P, 3, D])
        g2_bc = sb("g2_bc", [P, D])
        b2_bc = sb("b2_bc", [P, D])
        wr_sb = sb("wr_sb", [P, EXPERTS])
        br_row = sb("br_row", [1, EXPERTS])
        ones_row = sb("ones_row", [1, P])
        gelu_of_one = sb("gelu_of_one", [1, 1])
        w1_sb = sb("w1_sb", [P, EXPERTS, HID])
        w2_sb = sb("w2_sb", [P, EXPERTS, 2, D])
        fb1_bc = sb("fb1_bc", [P, EXPERTS, HID])
        fb2_bc = sb("fb2_bc", [P, EXPERTS, D])
        ident = sb("ident", [P, P])
        ident_b = sb("ident_b", [P, P], BF16)
        ones_b = sb("ones_b", [P, P], BF16)
        before_b = sb("before_b", [P, P], BF16)
        causal = sb("causal", [P, P])
        part_id = sb("part_id", [P, 1])
        expert_id = sb("expert_id", [P, EXPERTS])
        region_at = sb("region_at", [P, EXPERTS])
        tile_id = sb("tile_id", [P, FULL])
        zero_rows = sb("zero_rows", [P, ROW])

        onehot = sb("onehot", [ROWS_EMB, GROUPS, N])
        work_a = sb("work_a", [P, GROUPS, N])
        work_b = sb("work_b", [P, GROUPS, N])
        work_c = sb("work_c", [P, GROUPS, N])
        work_d = sb("work_d", [P, GROUPS, N])
        x1T = sb("x1T", [P, GROUPS, GS, PAD + L])
        h0 = sb("h0", [P, GROUPS, N])
        h1 = sb("h1", [P, GROUPS, N])
        spike_q = sb("spike_q", [P, GROUPS, N], BF16)
        spike_k = sb("spike_k", [P, GROUPS, N], BF16)
        spike_v = sb("spike_v", [P, GROUPS, N], BF16)
        routed = sb("routed", [P, GROUPS, N], BF16)
        stage = sb("stage", [P, TOPK, GROUPS, GS, ROW])
        LNS = 4
        WARM = 24
        stats = sb("stats", [P, LNS, GROUPS, GS, 6])
        mean_var = sb("mean_var", [P, LNS * GROUPS, GS, 2])
        rs_work = sb("rs_work", [P, 10, LNS * GROUPS, GS])
        logits = sb("logits", [P, GROUPS * GS, EXPERTS])
        top8 = sb("top8", [P, GROUPS * GS, 8])
        top8_at = sb("top8_at", [P, GROUPS * GS, 8], U32)
        chosen = sb("chosen", [P, GROUPS, TOPK, GS * EXPERTS])
        chosen_b = sb("chosen_b", [P, GROUPS, GS * EXPERTS], BF16)
        group_sum = sb("group_sum", [P, GROUPS, EXPERTS])
        chosen_sum = sb("chosen_sum", [P, GROUPS + 1, EXPERTS], BF16)
        rank_of = sb("rank_of", [P, GROUPS, TOPK, GS * EXPERTS])
        slot_f = sb("slot_f", [P, GROUPS, TOPK * GS])
        slot_of = sb("slot_of", [P, GROUPS, TOPK, GS], I32)
        shifted = sb("shifted", [P, GROUPS * GS, EXPERTS])
        exps = sb("exps", [P, GROUPS * GS, EXPERTS])
        top_shifted = sb("top_shifted", [P, GROUPS * GS, TOPK])
        top_exps = sb("top_exps", [P, GROUPS * GS, TOPK])
        top_probs = sb("top_probs", [P, GROUPS * GS, TOPK])
        w_work = sb("w_work", [P, 5, GROUPS * GS])
        w_top = sb("w_top", [P, GROUPS * GS, TOPK])

        count_i = sb("count_i", [P, EXPERTS], I32)
        tiles_i = sb("tiles_i", [P, EXPERTS], I32)
        tiles_f = sb("tiles_f", [P, EXPERTS])
        zeros_e = sb("zeros_e", [P, EXPERTS])
        tiles_upto = sb("tiles_upto", [P, EXPERTS])
        skip_rows = sb("skip_rows", [P, EXPERTS])
        done_before = sb("done_before", [P, FULL, EXPERTS])
        skipped = sb("skipped", [P, FULL, EXPERTS])
        tile_expert = sb("tile_expert", [P, FULL])
        tile_w = sb("tile_w", [P, FULL], I32)
        tile_skip = sb("tile_skip", [P, FULL])
        tile_row_f = sb("tile_row_f", [P, FULL])
        tile_row = sb("tile_row", [P, FULL], I32)
        tail_row = sb("tail_row", [P, EXPERTS], I32)

        xt = sb("xt", [P, U, ROW])
        xtT = sb("xtT", [P, 2, P])
        hid = sb("hid", [P, 2, HID])
        act_h = sb("act_h", [P, 2, HID])
        act_hT = sb("act_hT", [P, 2, HID])
        y_sb = work_a[:].rearrange("p g (s d) -> p (g s) d", d=D)

        ids_in, emb_in, rows_in, conv_in, qkv_in = map(sem, ("ids_in", "emb_in", "rows_in", "conv_in", "qkv_in"))
        gb2_in, router_in, w1_in, w2_in, fb_in = map(sem, ("gb2_in", "router_in", "w1_in", "w2_in", "fb_in"))
        consts_ready = sem("consts_ready")
        pool_chain, dve_chain = sem("pool_chain"), sem("dve_chain")
        ids_ready, ids_spread, onehot_ready = map(sem, ("ids_ready", "ids_spread", "onehot_ready"))
        cols_psum, cols_ready, qkvT_psum, qkvT_ready = map(sem, ("cols_psum", "cols_ready", "qkvT_psum", "qkvT_ready"))
        x0_psum, x0_used = sem("x0_psum"), sem("x0_used")
        stats_ready = [sem(f"stats{i}_ready") for i in range(LNS)]
        ln_ready = [sem(f"ln{i}_ready") for i in range(LNS)]
        normed = [sem(f"normed{i}") for i in range(LNS)]
        xhatT_psum, x1T_ready, convg_psum, conva_psum = map(sem, ("xhatT_psum", "x1T_ready", "convg_psum", "conva_psum"))
        tanh_ready, a_ready, glu_ready, z_psum, scaled_ready, h0_ready = map(
            sem, ("tanh_ready", "a_ready", "glu_ready", "z_psum", "scaled_ready", "h0_ready"))
        xaT_psum, xaT_ready, qkv_psum, spikes_ready = map(sem, ("xaT_psum", "xaT_ready", "qkv_psum", "spikes_ready"))
        score_psum, routed_ready, attn_psum, h1_ready = map(sem, ("score_psum", "routed_ready", "attn_psum", "h1_ready"))
        xfT_psum, xfT_ready, logits_psum = map(sem, ("xfT_psum", "xfT_ready", "logits_psum"))
        shifted_ready, exp_ready, chosen_ready, rank_psum, slots_ready = map(
            sem, ("shifted_ready", "exp_ready", "chosen_ready", "rank_psum", "slots_ready"))
        count_psum, count_ready, table_ready = map(sem, ("count_psum", "count_ready", "table_ready"))
        staged, spike_v_ready = sem("staged"), sem("spike_v_ready")
        rows_out, zeros_out, dummy_out = map(sem, ("rows_out", "zeros_out", "dummy_out"))
        xt_in = [sem(f"xt_in{i}") for i in range(U)]
        placed = [sem(f"placed{i}") for i in range(U)]
        t_xT_psum, t_xT, t_h_psum, t_h, t_act, t_actT_psum, t_actT, t_y_psum, t_y = map(
            sem, ("t_xT_psum", "t_xT", "t_h_psum", "t_h", "t_act", "t_actT_psum", "t_actT", "t_y_psum", "t_y"))
        parts_in = [[sem(f"parts{k}_in{g}") for g in range(GROUPS)] for k in range(TOPK)]
        base_ready, stored, scaled_y, summed, y_out = map(sem, ("base_ready", "stored", "scaled_y", "summed", "y_out"))

        def blocks(ap, s):
            return ap[:, s * P:(s + 1) * P]

        def by_seq(ap, n=P):
            return ap.rearrange("p (s n) -> p s n", n=n)

        EARLY = dict(x0=-2, weights=4, stats0=1, rsqrt0=2, ln0=5, xhatT=6, x1T=5, convg=9, conva=13, tanh=13, a=18)
        STAGES = dict(x1=13.5, glu=15, z=16, stats1=17, rsqrt1=17.1, ln1=19, scale=20, h0=20.5, stats2=21,
                      rsqrt2=23.1, ln2=23, xaT=27, xaTout=23.7, qkv=28, spikes=29, score=31, mask=32.5, attn=33.5,
                      h1out=31.7, stats3=34, rsqrt3=34.1, ln3=37, copy=43, xfT=38.5, xfTout=39,
                      logits=39.5, choose=41, rank=46, slot=49, scatter=56)
        EARLY_PERIOD, PERIOD = 13, 16

        def front(**program):
            order = [(start + EARLY_PERIOD * g, g, stage) for stage, start in EARLY.items() for g in range(GROUPS)]
            order += [(start + PERIOD * g, g, stage) for stage, start in STAGES.items() for g in range(GROUPS)]
            for _, g, stage in sorted(order):
                if stage in program:
                    program[stage](g)

        def norm_at(which, g):
            return slice(which * GROUPS + g, which * GROUPS + g + 1)

        def rsqrt(dve, link, at):
            v, y, y2, h, q, z, a, b = (rs_work[:, i, at, :] for i in range(8))
            link(dve.tensor_scalar(v, mean_var[:, at, :, 1], LN_EPS, None, ALU.add))
            link(dve.tensor_scalar(y.bitcast(I32), v.bitcast(I32), -0.5, RSQRT_SEED, ALU.mult, ALU.add))
            link(dve.tensor_tensor(y2, y, y, ALU.mult))
            link(dve.tensor_tensor(h, y2, v, ALU.mult))
            link(dve.scalar_tensor_tensor(out=q, in0=h, scalar=-10 / 3, in1=h, op0=ALU.add, op1=ALU.mult))
            link(dve.scalar_tensor_tensor(out=z, in0=q, scalar=5.0, in1=y, op0=ALU.add, op1=ALU.mult))
            link(dve.scalar_tensor_tensor(out=a, in0=z, scalar=-0.5 * 0.375 ** 3, in1=v, op0=ALU.mult, op1=ALU.mult))
            link(dve.tensor_tensor(b, a, z, ALU.mult))
            link(dve.scalar_tensor_tensor(out=rs_work[:, 8, at, :], in0=b, scalar=1.5 * 0.375, in1=z, op0=ALU.add,
                                          op1=ALU.mult))
            return dve.scalar_tensor_tensor(out=rs_work[:, 9, at, :], in0=mean_var[:, at, :, 0], scalar=-1.0,
                                            in1=rs_work[:, 8, at, :], op0=ALU.mult, op1=ALU.mult)

        def rsqrt_pool(pool, link, at):
            var, mean = mean_var[:, at, :, 1], mean_var[:, at, :, 0]
            v, y, y2, h, q, z, a, b, rstd, shift = (rs_work[:, i, at, :] for i in range(10))
            link(pool.tensor_scalar(v, var, LN_EPS, None, ALU.add))
            link(pool.tensor_scalar(y.bitcast(I32), v.bitcast(I32), -0.5, RSQRT_SEED, ALU.mult, ALU.add))
            link(pool.tensor_tensor(y2, y, y, ALU.mult))
            link(pool.tensor_tensor(h, y2, v, ALU.mult))
            link(pool.tensor_scalar(q, h, -10 / 3, None, ALU.add))
            link(pool.tensor_tensor(a, q, h, ALU.mult))
            link(pool.tensor_scalar(b, a, 5.0, None, ALU.add))
            link(pool.tensor_tensor(z, b, y, ALU.mult))
            link(pool.tensor_tensor(y2, z, z, ALU.mult))
            link(pool.tensor_tensor(h, y2, v, ALU.mult))
            link(pool.tensor_scalar(q, h, -0.5 * 0.375 ** 3, 1.5 * 0.375, ALU.mult, ALU.add))
            link(pool.tensor_tensor(rstd, q, z, ALU.mult))
            link(pool.tensor_tensor(a, mean, rstd, ALU.mult))
            return pool.tensor_scalar(shift, a, -1.0, None, ALU.mult)

        TILE_STEPS = dict(load_expert=0, turn_x=0, evacuate_x=0, first=1, add_b1=1, gelu=2, turn_act=3,
                          evacuate_act=3, second=4, add_b2=4)

        def experts(**program):
            for step in range(TILES + max(TILE_STEPS.values())):
                for name, run in program.items():
                    if 0 <= step - TILE_STEPS[name] < TILES:
                        run(step - TILE_STEPS[name])

        def experts_of(eng):
            of = {}

            def load_expert(j):
                if j < FULL:
                    e = eng.value_load(tile_w[0:1, j:j + 1], min_val=0, max_val=EXPERTS - 1)
                    of[j] = bass.ds(e, 1)
                else:
                    of[j] = slice(j - FULL, j - FULL + 1)
            return load_expert, of.__getitem__

        def flat(ap):
            return ap.rearrange("p o n -> p (o n)")

        work = dict(xhat=work_b, tanh=work_c, a=work_d, glu=work_a, zhat=work_b, scaled=work_c, xa=work_a,
                    xaT=work_b, xfT=work_d)

        def zero_fill(eng, e):
            n = eng.value_load(count_i[0:1, e:e + 1], min_val=0, max_val=T)
            eng.dma_start(slots[bass.ds(n + e * REGION, P), :], zero_rows[:]).then_inc(zeros_out, 16)

        block = ctx.enter_context(nc.Block())

        @block.sync
        def _(sp):
            sp.dma_start(ids_i[:], x).then_inc(ids_in, 16)
            sp.dma_start(emb_sb[:], emb).then_inc(emb_in, 16)
            sp.dma_start(pos_sb[:], pos).then_inc(emb_in, 16)
            for i, row in enumerate((g1, b1, conv_b[0:D], conv_b[D:2 * D])):
                sp.dma_start(rows4[i:i + 1, :], row.rearrange("(o n) -> o n", o=1)).then_inc(rows_in, 16)
            sp.dma_start(convw_sb[:], conv_w.rearrange("w i o -> i w o")).then_inc(conv_in, 16)
            for i, w in enumerate((Wq, Wk, Wv)):
                sp.dma_start(wqkv[:, i, :], w).then_inc(qkv_in, 16)
            sp.dma_start(g2_bc[:], g2.partition_broadcast(P)).then_inc(gb2_in, 16)
            sp.dma_start(b2_bc[:], b2.partition_broadcast(P)).then_inc(gb2_in, 16)
            sp.dma_start(wr_sb[:], Wr).then_inc(router_in, 16)
            sp.dma_start(br_row[:], br.rearrange("(o n) -> o n", o=1)).then_inc(router_in, 16)
            sp.dma_start(w1_sb[:], W1.rearrange("e d h -> d e h")).then_inc(w1_in, 16)
            sp.dma_start(w2_sb[:], W2.rearrange("e (c p) d -> p e c d", p=P)).then_inc(w2_in, 16)
            sp.dma_start(fb1_bc[:].rearrange("p e h -> p (e h)"),
                         fb1.rearrange("e h -> (e h)").partition_broadcast(P)).then_inc(fb_in, 16)
            sp.dma_start(fb2_bc[:].rearrange("p e d -> p (e d)"),
                         fb2.rearrange("e d -> (e d)").partition_broadcast(P)).then_inc(fb_in, 16)
            sp.wait_ge(consts_ready, 2)
            sp.dma_start(slots[DUMMY:DUMMY + P, :], zero_rows[:]).then_inc(dummy_out, 16)

            sp.wait_ge(count_ready, 1)
            for e in range(EXPERTS // 2):
                zero_fill(sp, e)

            sp.wait_ge(table_ready, 1)
            sp.wait_ge(dummy_out, 16)
            for j in range(TILES):
                u = j % U
                if j < FULL:
                    row = sp.value_load(tile_row[0:1, j:j + 1], min_val=0, max_val=DUMMY)
                else:
                    row = sp.value_load(tail_row[0:1, j - FULL:j - FULL + 1], min_val=0, max_val=DUMMY - P)
                if j == 0:
                    sp.wait_ge(rows_out, 16 * TOPK * SEQS)
                if j == FULL:
                    sp.wait_ge(zeros_out, 16 * EXPERTS)
                if j >= U:
                    sp.wait_ge(placed[u], 16 * (j // U))
                sp.dma_start(xt[:, u, :], slots[bass.ds(row, P), :]).then_inc(xt_in[u], 16)

            for u in range(U):
                sp.wait_ge(placed[u], 16 * (TILES // U))
            both = parts.rearrange("(k b p) d -> k p b d", k=TOPK, p=P)
            for k, buf in ((1, work_b), (0, work_a)):
                for g in range(GROUPS):
                    sp.dma_start(by_seq(buf[:, g, :]), both[k, :, g * GS:(g + 1) * GS, :]).then_inc(parts_in[k][g], 16)
            tokens = out.rearrange("b t d -> t b d")
            for g in range(GROUPS):
                sp.wait_ge(y_out, g + 1)
                sp.dma_start(tokens[:, g * GS:(g + 1) * GS, :],
                             by_seq(work_c[:, g, :])).then_inc(stored, 16)
            sp.wait_ge(stored, 16 * GROUPS)

        @block.gpsimd
        def _(pool):
            done = [0]

            def link(ins):
                done[0] += 1
                ins.then_inc(pool_chain, 1)
                pool.wait_ge(pool_chain, done[0])

            link(pool.memset(ident[:], 0.0))
            pool.iota(part_id[:], pattern=[[0, 1]], base=0, channel_multiplier=1, allow_small_or_imprecise_dtypes=True)
            link(pool.affine_select(out=ident[:], in_=ident[:], compare_op=ALU.not_equal, fill=1.0, base=0,
                                    pattern=[[-1, P]], channel_multiplier=1))
            pool.tensor_copy(ident_b[:], ident[:]).then_inc(consts_ready, 1)

            pool.memset(x1T[:, :, :, 0:PAD], 0.0)
            pool.memset(ones_b[:], 1.0)
            pool.memset(ones_row[:], 1.0)
            pool.memset(zero_rows[:], 0.0)
            pool.memset(zeros_e[:], 0.0)
            pool.memset(causal[:], 1.0)
            pool.memset(stage[:, :, :, :, D:], 0.0)
            link(pool.memset(chosen_sum[:, 0, :], 0.0))
            pool.affine_select(out=causal[:], in_=causal[:], compare_op=ALU.is_ge, fill=0.0, base=0,
                               pattern=[[1, P]], channel_multiplier=-1)
            pool.affine_select(out=before_b[:], in_=ones_b[:], compare_op=ALU.is_gt, fill=0.0, base=0,
                               pattern=[[1, P]], channel_multiplier=-1)
            pool.iota(expert_id[:], pattern=[[1, EXPERTS]], base=0, channel_multiplier=0,
                      allow_small_or_imprecise_dtypes=True)
            pool.iota(region_at[:], pattern=[[REGION, EXPERTS]], base=0, channel_multiplier=0,
                      allow_small_or_imprecise_dtypes=True)
            pool.iota(tile_id[:], pattern=[[1, FULL]], base=0, channel_multiplier=0,
                      allow_small_or_imprecise_dtypes=True)
            for k in range(TOPK):
                pool.iota(stage[:, k, :, :, ROW_PLACE:ROW_PLACE + 1].bitcast(I32),
                          pattern=[[N, GROUPS], [P, GS], [0, 1]], base=k * T, channel_multiplier=1)
            pool.memset(zero_rows[:, ROW_PLACE:ROW_PLACE + 1].bitcast(I32), NOWHERE).then_inc(consts_ready, 1)
            pool.wait_ge(consts_ready, 2)

            def rsqrt_x0(g):
                if g >= 1:
                    pool.wait_ge(stats_ready[0], g + 1)
                    rsqrt_pool(pool, link, norm_at(0, g)).then_inc(ln_ready[0], 1)

            def scale_g2(g):
                if g == 0:
                    pool.wait_ge(gb2_in, 32)
                for half in range(0, GS, GS // 2):
                    pool.wait_ge(normed[1], GS * g + half + GS // 2)
                    last = pool.tensor_tensor(
                        by_seq(work["scaled"][:, g, :])[:, half:half + GS // 2, :],
                        by_seq(work["zhat"][:, g, :])[:, half:half + GS // 2, :],
                        g2_bc[:].unsqueeze(1).broadcast_to([P, GS // 2, D]), ALU.mult)
                last.then_inc(scaled_ready, 1)

            def scatter_rows(g):
                pool.wait_ge(staged, g + 1)
                pool.wait_ge(slots_ready, g + 1)
                for s in range(GS):
                    for k in range(TOPK):
                        pool.indirect_dma_start(
                            out=slots, out_offset=bass.IndirectOffsetOnAxis(
                                ap=slot_of[:, g, k, s:s + 1].bitcast(U32), axis=0),
                            in_=stage[:, k, g, s, :], in_offset=None).then_inc(rows_out, 16)

            front(rsqrt0=rsqrt_x0, scale=scale_g2, scatter=scatter_rows)

            last_place = pool.to_reg(TOPK * T - 1)

            for j in range(TILES):
                u = j % U
                pool.wait_ge(t_y, j + 1)
                pool.indirect_dma_start(
                    out=parts, out_offset=bass.IndirectOffsetOnAxis(
                        ap=xt[:, u, ROW_PLACE:ROW_PLACE + 1].bitcast(U32), axis=0),
                    in_=y_sb[:, u, :], in_offset=None, bounds_check=last_place,
                    oob_is_err=False).then_inc(placed[u], 16)

            pool.wait_ge(base_ready, 1)
            for g in range(GROUPS):
                pool.wait_ge(scaled_y, g + 1)
                most = slice(0, (GS - 1) * P)
                pool.tensor_tensor(work_d[:, g, most], work_c[:, g, most], h0[:, g, most], ALU.add).then_inc(summed, 1)

        @block.scalar
        def _(act):
            def weights(g):
                if g == 0:
                    act.wait_ge(cols_psum, 1)
                    act.activation(cols4[:, 0:2], bank[7][:, 0:2], ACT.Copy)
                    act.activation(cols4[:, 2:4], bank[7][:, 2:4], ACT.Copy, scale=0.5).then_inc(cols_ready, 1)
                    act.wait_ge(qkvT_psum, 1)
                    act.activation(wqkvT[:].rearrange("p w n -> p (w n)"), bank[6][:, 0:3 * D],
                                   ACT.Copy).then_inc(qkvT_ready, 1)
                    act.wait_ge(cols_ready, 1)

            def normalise(g, which, src, dst):
                act.wait_ge(ln_ready[which], g + 1)
                at = which * GROUPS + g
                for s in range(GS):
                    act.activation(dst[s], src[s], ACT.Identity, scale=rs_work[:, 8, at, s:s + 1],
                                   bias=rs_work[:, 9, at, s:s + 1]).then_inc(normed[which], 1)

            def parts_of(buf, g):
                return [blocks(buf[:, g, :], s) for s in range(GS)]

            def norm_x0(g):
                normalise(g, 0, [blocks(bank[0], s) for s in range(GS)], parts_of(work["xhat"], g))

            def evacuate_x1T(g):
                act.wait_ge(xhatT_psum, g + 1)
                act.activation(x1T[:, g, :, PAD:], by_seq(bank[0][:]), ACT.Identity, scale=cols4[:, 0:1],
                               bias=cols4[:, 1:2]).then_inc(x1T_ready, 1)

            def gate_tanh(g):
                act.wait_ge(convg_psum, g + 1)
                act.activation(work["tanh"][:, g, :], bank[2][:], ACT.Tanh, scale=0.5,
                               bias=cols4[:, 3:4]).then_inc(tanh_ready, 1)

            def gate_a(g):
                act.wait_ge(conva_psum, g + 1)
                act.activation(work["a"][:, g, :], bank[3][:], ACT.Identity, scale=0.5,
                               bias=cols4[:, 2:3]).then_inc(a_ready, 1)

            def norm_z(g):
                normalise(g, 1, [blocks(bank[1], s) for s in range(GS)], parts_of(work["zhat"], g))

            def norm_h0(g):
                normalise(g, 2, parts_of(h0, g), parts_of(work["xa"], g))

            def evacuate_xaT(g):
                act.wait_ge(xaT_psum, g + 1)
                act.activation(work["xaT"][:, g, :], bank[1][:], ACT.Copy).then_inc(xaT_ready, 1)

            def evacuate_h1(g):
                act.wait_ge(attn_psum, g + 1)
                act.activation(h1[:, g, :], bank[4][:], ACT.Copy).then_inc(h1_ready, 1)

            def norm_h1(g):
                normalise(g, 3, parts_of(h1, g), [stage[:, 0, g, s, 0:D] for s in range(GS)])

            def copy_rows(g):
                act.wait_ge(normed[3], GS * (g + 1))
                act.activation(stage[:, 1, g, :, 0:D], stage[:, 0, g, :, 0:D], ACT.Copy).then_inc(staged, 1)

            def evacuate_xfT(g):
                act.wait_ge(xfT_psum, g + 1)
                act.activation(work["xfT"][:, g, :], bank[6][:], ACT.Copy).then_inc(xfT_ready, 1)

            front(weights=weights, ln0=norm_x0, x1T=evacuate_x1T, tanh=gate_tanh, a=gate_a, ln1=norm_z,
                  ln2=norm_h0, xaTout=evacuate_xaT, h1out=evacuate_h1, ln3=norm_h1, copy=copy_rows,
                  xfTout=evacuate_xfT)

            act.wait_ge(count_ready, 1)
            for e in range(EXPERTS // 2, EXPERTS):
                zero_fill(act, e)

            act.wait_ge(shifted_ready, 1)
            act.activation(exps[:], shifted[:], ACT.Exp)
            act.activation(top_exps[:], top_shifted[:], ACT.Exp).then_inc(exp_ready, 1)
            act.activation(gelu_of_one[:], ones_row[:, 0:1], ACT.Gelu)

            def evacuate_x(j):
                b = j % 2
                act.wait_ge(t_xT_psum, j + 1)
                act.activation(xtT[:, b, :], bank[b][:, 0:P], ACT.Copy).then_inc(t_xT, 1)

            def gelu(j):
                b = j % 2
                act.wait_ge(t_h, j + 1)
                act.activation(act_h[:, b, :], hid[:, b, :], ACT.Gelu).then_inc(t_act, 1)

            def evacuate_act(j):
                b = j % 2
                act.wait_ge(t_actT_psum, j + 1)
                act.activation(act_hT[:, b, :], bank[4 + b][:, 0:HID], ACT.Copy).then_inc(t_actT, 1)

            experts(evacuate_x=evacuate_x, evacuate_act=evacuate_act, gelu=gelu)

            act.wait_ge(base_ready, 1)
            for g in range(GROUPS):
                act.wait_ge(parts_in[1][g], 16)
                for s in range(GS - 1):
                    last = act.activation(blocks(work_c[:, g, :], s), blocks(work_b[:, g, :], s), ACT.Identity,
                                          scale=w_top[:, g * GS + s, 1:2])
                last.then_inc(scaled_y, 1)

        @block.vector
        def _(dve):
            done = [0]

            def link(ins):
                done[0] += 1
                ins.then_inc(dve_chain, 1)
                dve.wait_ge(dve_chain, done[0])

            def mark(ins):
                done[0] += 1
                ins.then_inc(dve_chain, 1)
                return done[0]

            dve.wait_ge(ids_in, 16)
            link(dve.tensor_scalar(ids_f[:, 0, :], ids_i[:], 0.0, float(ROWS_EMB), ALU.is_lt, ALU.mult))
            link(dve.tensor_tensor(ids_f[:, 1, :], ids_f[:, 0, :], ids_i[:], ALU.add))
            dve.tensor_scalar(ids_b[:], ids_f[:, 1, :], 0.0, float(ROWS_EMB - 1), ALU.max,
                              ALU.min).then_inc(ids_ready, 1)
            dve.wait_ge(consts_ready, 1)
            def find_rows(g):
                dve.wait_ge(ids_spread, g + 1)
                dve.tensor_scalar(onehot[:, g, :], bank[2 + g][0:ROWS_EMB, :], part_id[0:ROWS_EMB, :], None,
                                  ALU.is_equal).then_inc(onehot_ready, 1)

            find_rows(0)

            def layer_stats(g, which, src):
                made = [mark(dve.bn_stats(stats[:, which, g, s, :], blocks(src, s))) for s in range(GS)]
                for s in range(GS):
                    dve.wait_ge(dve_chain, made[s])
                    last = dve.bn_aggr(mean_var[:, which * GROUPS + g, s, :], stats[:, which, g, s, :])
                last.then_inc(stats_ready[which], 1)

            def scale_and_shift(which, g):
                dve.wait_ge(stats_ready[which], g + 1)
                rsqrt(dve, link, norm_at(which, g)).then_inc(ln_ready[which], 1)

            def stats_x0(g):
                if g == 1:
                    dve.wait_ge(consts_ready, 2)
                dve.wait_ge(x0_psum, g + 1)
                layer_stats(g, 0, bank[0])

            def rsqrt_x0(g):
                if g == 0:
                    scale_and_shift(0, g)
                    for later in range(1, GROUPS):
                        find_rows(later)

            def glu(g):
                dve.wait_ge(tanh_ready, g + 1)
                dve.wait_ge(a_ready, g + 1)
                dve.scalar_tensor_tensor(out=work["glu"][:, g, :], in0=work["tanh"][:, g, :], scalar=1.0,
                                         in1=work["a"][:, g, :], op0=ALU.add, op1=ALU.mult).then_inc(glu_ready, 1)

            def stats_z(g):
                dve.wait_ge(z_psum, g + 1)
                layer_stats(g, 1, bank[1])

            def rsqrt_z(g):
                scale_and_shift(1, g)

            def make_h0(g):
                dve.wait_ge(scaled_ready, g + 1)
                dve.tensor_tensor(by_seq(h0[:, g, :]), by_seq(work["scaled"][:, g, :]),
                                  b2_bc[:].unsqueeze(1).broadcast_to([P, GS, D]), ALU.add).then_inc(h0_ready, 1)

            def stats_h0(g):
                dve.wait_ge(h0_ready, g + 1)
                layer_stats(g, 2, h0[:, g, :])

            def rsqrt_h0(g):
                scale_and_shift(2, g)

            def spikes(g):
                dve.wait_ge(qkv_psum, 3 * g + 1)
                dve.tensor_scalar(spike_q[:, g, :], bank[4][:], Q_THRESH, None, ALU.is_ge)
                dve.wait_ge(qkv_psum, 3 * g + 2)
                dve.tensor_scalar(spike_k[:, g, :], bank[5][:], K_THRESH, None, ALU.is_ge).then_inc(spikes_ready, 1)
                dve.wait_ge(qkv_psum, 3 * g + 3)
                dve.tensor_scalar(spike_v[:, g, :], bank[6][:], V_THRESH, None, ALU.is_ge).then_inc(spike_v_ready, 1)

            def route_mask(g):
                dve.wait_ge(score_psum, g + 1)
                dve.scalar_tensor_tensor(out=by_seq(routed[:, g, :]), in0=by_seq(bank[5][:]), scalar=MASK_THRESH,
                                         in1=causal[:].unsqueeze(1).broadcast_to([P, GS, P]), op0=ALU.is_gt,
                                         op1=ALU.mult).then_inc(routed_ready, 1)

            def stats_h1(g):
                dve.wait_ge(h1_ready, g + 1)
                layer_stats(g, 3, h1[:, g, :])

            def rsqrt_h1(g):
                scale_and_shift(3, g)

            def by_expert(ap):
                return ap.rearrange("p (s e) -> p s e", e=EXPERTS)

            def choose(g):
                dve.wait_ge(logits_psum, g + 1)
                seqs = slice(g * GS, (g + 1) * GS)
                fresh = bank[7][:, 0:GS * EXPERTS].rearrange("p (s e) -> p s e", e=EXPERTS)
                made = [mark(dve.max(top8[:, g * GS + s, :], fresh[:, s, :])) for s in range(GS)]
                for s in range(GS):
                    dve.wait_ge(dve_chain, made[s])
                    last = dve.max_index(top8_at[:, g * GS + s, :], top8[:, g * GS + s, :], fresh[:, s, :])
                dve.tensor_copy(logits[:, seqs, :], fresh)
                link(last)
                both = [P, TOPK, GS, EXPERTS]
                link(dve.tensor_tensor(chosen[:, g, :, :].rearrange("p k (s e) -> p k s e", e=EXPERTS),
                                       expert_id[:].unsqueeze(1).unsqueeze(1).broadcast_to(both),
                                       top8_at[:, seqs, 0:TOPK].rearrange("p s k -> p k s").unsqueeze(3)
                                       .broadcast_to(both), ALU.is_equal))
                dve.tensor_tensor(chosen_b[:, g, :], chosen[:, g, 0, :], chosen[:, g, 1, :],
                                  ALU.add).then_inc(chosen_ready, 1)
                dve.wait_ge(chosen_ready, 2 * g + 1)
                counts = chosen_b[:, g, :].rearrange("p (s e) -> p e s", e=EXPERTS)
                link(dve.tensor_reduce(group_sum[:, g, :], counts, AX_X, ALU.add))
                dve.tensor_tensor(chosen_sum[:, g + 1, :], group_sum[:, g, :], chosen_sum[:, g, :],
                                  ALU.add).then_inc(chosen_ready, 1)

            def slots_of(g):
                dve.wait_ge(rank_psum, g + 1)
                link(dve.tensor_tensor(rank_of[:, g, :, :], chosen[:, g, :, :],
                                       bank[7][:, 64:64 + GS * EXPERTS].unsqueeze(1)
                                       .broadcast_to([P, TOPK, GS * EXPERTS]), ALU.mult))
                link(dve.tensor_reduce(slot_f[:, g, :], rank_of[:, g, :, :].rearrange("p k (s e) -> p (k s) e", e=EXPERTS),
                                       AX_X, ALU.add))
                dve.tensor_copy(slot_of[:, g, :, :].rearrange("p k s -> p (k s)"),
                                slot_f[:, g, :]).then_inc(slots_ready, 1)

            front(stats0=stats_x0, rsqrt0=rsqrt_x0, glu=glu, stats1=stats_z, rsqrt1=rsqrt_z, h0=make_h0,
                  stats2=stats_h0, rsqrt2=rsqrt_h0, spikes=spikes, mask=route_mask, stats3=stats_h1, rsqrt3=rsqrt_h1,
                  choose=choose, slot=slots_of)

            dve.wait_ge(count_psum, 1)
            dve.tensor_copy(count_i[:], bank[7][:, 128:128 + EXPERTS]).then_inc(count_ready, 1)
            dve.wait_ge(count_ready, 1)
            link(dve.tensor_scalar(tiles_i[:], count_i[:], P.bit_length() - 1, None, ALU.logical_shift_right))
            link(dve.tensor_copy(tiles_f[:], tiles_i[:]))
            dve.tensor_scalar(skip_rows[:], tiles_f[:], -float(P), float(REGION), ALU.mult, ALU.add)
            dve.scalar_tensor_tensor(out=tail_row[:], in0=tiles_f[:], scalar=float(P), in1=region_at[:], op0=ALU.mult,
                                     op1=ALU.add)
            link(dve.tensor_tensor_scan(tiles_upto[:], tiles_f[:], zeros_e[:], 0.0, ALU.add, ALU.add))
            every = [P, FULL, EXPERTS]
            link(dve.tensor_tensor(done_before[:], tile_id[:].unsqueeze(2).broadcast_to(every),
                                   tiles_upto[:].unsqueeze(1).broadcast_to(every), ALU.is_ge))
            dve.tensor_tensor(skipped[:], done_before[:], skip_rows[:].unsqueeze(1).broadcast_to(every), ALU.mult)
            link(dve.tensor_reduce(tile_expert[:], done_before[:], AX_X, ALU.add))
            link(dve.tensor_reduce(tile_skip[:], skipped[:], AX_X, ALU.add))
            dve.tensor_scalar(tile_w[:], tile_expert[:], float(EXPERTS - 1), None, ALU.min)
            link(dve.scalar_tensor_tensor(out=tile_row_f[:], in0=tile_id[:], scalar=float(P), in1=tile_skip[:],
                                          op0=ALU.mult, op1=ALU.add))
            dve.tensor_scalar(tile_row[:], tile_row_f[:], float(DUMMY), None, ALU.min).then_inc(table_ready, 1)

            largest = top8[:, :, 0:1]
            dve.tensor_tensor(shifted[:], logits[:], largest.broadcast_to([P, GROUPS * GS, EXPERTS]), ALU.subtract)
            dve.tensor_tensor(top_shifted[:], top8[:, :, 0:TOPK], largest.broadcast_to([P, GROUPS * GS, TOPK]),
                              ALU.subtract).then_inc(shifted_ready, 1)

            dve.wait_ge(h1_ready, GROUPS)
            for g in range(GROUPS):
                last = dve.tensor_tensor(by_seq(h0[:, g, :]), by_seq(h1[:, g, :]), stage[:, 0, g, :, 0:D], ALU.add)
            link(last)

            dve.wait_ge(exp_ready, 1)
            link(dve.tensor_reduce(w_work[:, 0, :], exps[:], AX_X, ALU.add))
            link(dve.reciprocal(w_work[:, 1, :], w_work[:, 0, :]))
            link(dve.tensor_tensor(top_probs[:], top_exps[:],
                                   w_work[:, 1, :].unsqueeze(2).broadcast_to([P, GROUPS * GS, TOPK]), ALU.mult))
            link(dve.tensor_tensor(w_work[:, 2, :], top_probs[:, :, 0], top_probs[:, :, 1], ALU.add))
            link(dve.tensor_scalar(w_work[:, 3, :], w_work[:, 2, :], TOPK_FLOOR, None, ALU.max))
            link(dve.reciprocal(w_work[:, 4, :], w_work[:, 3, :]))
            dve.tensor_tensor(w_top[:], top_probs[:],
                                   w_work[:, 4, :].unsqueeze(2).broadcast_to([P, GROUPS * GS, TOPK]),
                                   ALU.mult).then_inc(base_ready, 1)

            dve.wait_ge(table_ready, 1)
            dve.wait_ge(fb_in, 32)
            load_expert, expert_of = experts_of(dve)

            def add_b1(j):
                b = j % 2
                dve.wait_ge(t_h_psum, j + 1)
                dve.tensor_tensor(hid[:, b, :], bank[2 + b][:, 0:HID], flat(fb1_bc[:, expert_of(j), :]),
                                  ALU.add).then_inc(t_h, 1)

            def add_b2(j):
                u, b = j % U, j % 2
                dve.wait_ge(t_y_psum, j + 1)
                dve.tensor_tensor(y_sb[:, u, :], bank[6 + b][:, 0:D], flat(fb2_bc[:, expert_of(j), :]),
                                  ALU.add).then_inc(t_y, 1)

            experts(load_expert=load_expert, add_b2=add_b2, add_b1=add_b1)

            dve.wait_ge(base_ready, 1)
            for g in range(GROUPS):
                dve.wait_ge(parts_in[1][g], 16)
                last = dve.scalar_tensor_tensor(
                    out=blocks(work_d[:, g, :], GS - 1), in0=blocks(work_b[:, g, :], GS - 1),
                    scalar=w_top[:, g * GS + GS - 1, 1:2], in1=blocks(h0[:, g, :], GS - 1), op0=ALU.mult, op1=ALU.add)
            link(last)
            for g in range(GROUPS):
                dve.wait_ge(parts_in[0][g], 16)
                dve.wait_ge(summed, g + 1)
                for s in range(GS):
                    last = dve.scalar_tensor_tensor(
                        out=blocks(work_c[:, g, :], s), in0=blocks(work_a[:, g, :], s), scalar=w_top[:, g * GS + s, 0:1],
                        in1=blocks(work_d[:, g, :], s), op0=ALU.mult, op1=ALU.add)
                last.then_inc(y_out, 1)

        @block.tensor
        def _(pe):
            pe.wait_ge(consts_ready, 1)
            def begin_x0(g):
                if g == 0:
                    pe.wait_ge(emb_in, 32)
                else:
                    pe.wait_ge(x1T_ready, g)
                pe.matmul(by_seq(bank[0][:]), ident[:], pos_sb[:].unsqueeze(1).broadcast_to([P, GS, D]),
                          start=True, stop=False)

            def spread_ids(g):
                for s in range(GS):
                    b = g * GS + s
                    last = pe.matmul(blocks(bank[2 + g][0:ROWS_EMB, :], s),
                                     ident_b[0:SEQS, b:b + 1].broadcast_to([SEQS, ROWS_EMB]), ids_b[:],
                                     start=True, stop=True)
                last.then_inc(ids_spread, 1)

            pe.wait_ge(ids_ready, 1)
            spread_ids(0)
            begin_x0(0)

            def weights(g):
                if g == 0:
                    pe.wait_ge(rows_in, 64)
                    pe.transpose(bank[7][:, 0:4], rows4[:], ident[0:4, 0:4]).then_inc(cols_psum, 1)
                    pe.wait_ge(qkv_in, 48)
                    for i in range(3):
                        last = pe.transpose(bank[6][:, i * D:(i + 1) * D], wqkv[:, i, :], ident[:])
                    last.then_inc(qkvT_psum, 1)
                    pe.wait_ge(consts_ready, 2)

            def turn(dst, src, which, g):
                for s in range(GS):
                    pe.wait_ge(normed[which], GS * g + s + 1)
                    last = pe.transpose(blocks(dst, s), src[s], ident[:])
                return last

            def parts_of(buf, g):
                return [blocks(buf[:, g, :], s) for s in range(GS)]

            def lookup(g):
                if g >= 1:
                    begin_x0(g)
                pe.wait_ge(onehot_ready, g + 1)
                for s in range(GS):
                    last = pe.matmul(blocks(bank[0], s), blocks(onehot[:, g, :], s), emb_sb[:], start=False,
                                     stop=(s == GS - 1))
                last.then_inc(x0_psum, 1)
                if g == 0:
                    for later in range(1, GROUPS):
                        spread_ids(later)

            def turn_xhat(g):
                pe.wait_ge(normed[0], GS * (g + 1))
                turn(bank[0], parts_of(work["xhat"], g), 0, g).then_inc(xhatT_psum, 1)

            def conv(half, g, free, full):
                if g == 0:
                    pe.wait_ge(conv_in, 16)
                    pe.wait_ge(onehot_ready, GROUPS)
                pe.wait_ge(x1T_ready, g + 1)
                if g >= 1:
                    pe.wait_ge(free, g)
                acc = bank[3 - half]
                for w in range(TAPS):
                    last = pe.matmul(by_seq(acc[:]), convw_sb[:, w, half * D:(half + 1) * D],
                                     x1T[:, g, :, w:w + L], start=(w == 0), stop=(w == TAPS - 1))
                last.then_inc(full, 1)

            def conv_gate(g):
                conv(1, g, tanh_ready, convg_psum)

            def conv_a(g):
                conv(0, g, a_ready, conva_psum)

            def add_x1(g):
                pe.wait_ge(x1T_ready, g + 1)
                if g >= 1:
                    pe.wait_ge(xaT_ready, g)
                for s in range(GS):
                    pe.matmul(blocks(bank[1], s), x1T[:, g, s, PAD:], ident[:], start=(s == 0), stop=False)

            def add_glu(g):
                pe.wait_ge(glu_ready, g + 1)
                for s in range(GS):
                    last = pe.matmul(blocks(bank[1], s), blocks(work["glu"][:, g, :], s), ident[:], start=False,
                                     stop=(s == GS - 1))
                last.then_inc(z_psum, 1)

            def turn_xa(g):
                pe.wait_ge(normed[1], GS * (g + 1))
                turn(bank[1], parts_of(work["xa"], g), 2, g).then_inc(xaT_psum, 1)

            def project(g):
                if g == 0:
                    pe.wait_ge(qkvT_ready, 1)
                pe.wait_ge(xaT_ready, g + 1)
                if g >= 1:
                    pe.wait_ge(h1_ready, g)
                    pe.wait_ge(xfT_ready, g)
                xaT = work["xaT"][:, g, :]
                pe.matmul(bank[4][:], wqkvT[:, 0, :], xaT, start=True, stop=True).then_inc(qkv_psum, 1)
                pe.matmul(bank[5][:], wqkvT[:, 1, :], xaT, start=True, stop=True).then_inc(qkv_psum, 1)
                for s in range(GS):
                    last = pe.matmul(blocks(bank[6], s), blocks(xaT, s), wqkvT[:, 2, :], start=True, stop=True)
                last.then_inc(qkv_psum, 1)

            def score(g):
                pe.wait_ge(spikes_ready, g + 1)
                for s in range(GS):
                    last = pe.matmul(blocks(bank[5], s), blocks(spike_k[:, g, :], s), blocks(spike_q[:, g, :], s),
                                     start=True, stop=True)
                last.then_inc(score_psum, 1)
                pe.matmul(bank[4][:], ident[:], h0[:, g, :], start=True, stop=False)

            def attend(g):
                pe.wait_ge(spike_v_ready, g + 1)
                pe.wait_ge(routed_ready, g + 1)
                for s in range(GS):
                    last = pe.matmul(blocks(bank[4], s), blocks(routed[:, g, :], s), blocks(spike_v[:, g, :], s),
                                     start=False, stop=(s == GS - 1))
                last.then_inc(attn_psum, 1)

            def turn_xf(g):
                turn(bank[6], [stage[:, 0, g, s, 0:D] for s in range(GS)], 3, g).then_inc(xfT_psum, 1)

            def router(g):
                if g == 0:
                    pe.wait_ge(router_in, 32)
                pe.wait_ge(xfT_ready, g + 1)
                if g >= 1:
                    pe.wait_ge(slots_ready, g)
                pe.matmul(bank[7][:, 0:GS * EXPERTS].rearrange("p (s e) -> p s e", e=EXPERTS), ones_row[:],
                          br_row[:].unsqueeze(1).broadcast_to([1, GS, EXPERTS]), start=True, stop=False)
                for s in range(GS):
                    last = pe.matmul(bank[7][:, s * EXPERTS:(s + 1) * EXPERTS], blocks(work["xfT"][:, g, :], s),
                                     wr_sb[:], start=False, stop=(s == GS - 1))
                last.then_inc(logits_psum, 1)

            def rank(g):
                pe.wait_ge(chosen_ready, 2 * g + 1)
                ranks = bank[7][:, 64:64 + GS * EXPERTS]
                pe.matmul(ranks.rearrange("p (s e) -> p s e", e=EXPERTS), ones_row[:],
                          region_at[0:1, :].unsqueeze(1).broadcast_to([1, GS, EXPERTS]), start=True, stop=False)
                pe.matmul(ranks, before_b[:], chosen_b[:, g, :], start=False, stop=False)
                for s in range(GS - 1):
                    behind = GS - 1 - s
                    pe.matmul(ranks[:, (s + 1) * EXPERTS:].rearrange("p (s e) -> p s e", e=EXPERTS), ones_b[:],
                              chosen_b[:, g, s * EXPERTS:(s + 1) * EXPERTS].unsqueeze(1)
                              .broadcast_to([P, behind, EXPERTS]), start=False, stop=False)
                pe.matmul(ranks.rearrange("p (s e) -> p s e", e=EXPERTS), ones_b[:],
                          chosen_sum[:, g, :].unsqueeze(1).broadcast_to([P, GS, EXPERTS]),
                          start=False, stop=True).then_inc(rank_psum, 1)
                if g == GROUPS - 1:
                    pe.wait_ge(slots_ready, GROUPS)
                    pe.matmul(bank[7][:, 128:128 + EXPERTS], ones_b[:], chosen_sum[:, GROUPS, :],
                              start=True, stop=True).then_inc(count_psum, 1)

            front(weights=weights, x0=lookup, xhatT=turn_xhat, convg=conv_gate, conva=conv_a, x1=add_x1, z=add_glu,
                  xaT=turn_xa, qkv=project, score=score, attn=attend, xfT=turn_xf, logits=router, rank=rank)

            pe.wait_ge(table_ready, 1)
            for _ in range(WARM):
                pe.matmul(bank[5][:], ident_b[:], ones_b[:].unsqueeze(1).broadcast_to([P, 4, P]), start=True, stop=True)
            pe.wait_ge(w1_in, 16)
            pe.wait_ge(w2_in, 16)

            load_expert, expert_of = experts_of(pe)

            def turn_x(j):
                u, b = j % U, j % 2
                pe.wait_ge(xt_in[u], 16 * (j // U + 1))
                pe.transpose(bank[b][:, 0:P], xt[:, u, 0:D], ident[:]).then_inc(t_xT_psum, 1)

            def first(j):
                b = j % 2
                pe.wait_ge(t_xT, j + 1)
                pe.matmul(bank[2 + b][:, 0:HID], xtT[:, b, :], flat(w1_sb[:, expert_of(j), :]),
                          start=True, stop=True).then_inc(t_h_psum, 1)

            def turn_act(j):
                b = j % 2
                pe.wait_ge(t_act, j + 1)
                for c in range(2):
                    last = pe.transpose(bank[4 + b][:, c * P:(c + 1) * P], act_h[:, b, c * P:(c + 1) * P], ident[:])
                last.then_inc(t_actT_psum, 1)

            def second(j):
                b = j % 2
                pe.wait_ge(t_actT, j + 1)
                if j == TILES - 1:
                    pe.wait_ge(t_y, j - 1)
                for c in range(2):
                    last = pe.matmul(bank[6 + b][:, 0:D], act_hT[:, b, c * P:(c + 1) * P],
                                     flat(w2_sb[:, expert_of(j), c, :]), start=(c == 0), stop=(c == 1))
                last.then_inc(t_y_psum, 1)

            experts(load_expert=load_expert, turn_x=turn_x, turn_act=turn_act, second=second, first=first)


_INS = ["x", "fside_BS_emb", "L0_tok_pos", "L0_tok_g1", "L0_tok_b1", "L0_tok_conv_w", "L0_tok_conv_b", "L0_tok_g2",
        "L0_tok_b2", "L0_attn_Wq", "L0_attn_Wk", "L0_attn_Wv", "L0_ffn_Wr", "L0_ffn_br", "L0_ffn_W1", "L0_ffn_b1",
        "L0_ffn_W2", "L0_ffn_b2"]


def kernel(**inputs):
    import numpy as _np
    import concourse.bacc as _bacc
    from concourse import mybir as _mybir
    from concourse.bass_utils import run_bass_kernel_spmd as _run

    nc = _bacc.Bacc("TRN2", target_bir_lowering=False, num_devices=1)
    arrays, args = {}, []
    for name in _INS:
        a = _np.ascontiguousarray(inputs[name])
        arrays[f"in_{name}_dram"] = a
        args.append(nc.dram_tensor(f"in_{name}_dram", a.shape, _mybir.dt.from_np(a.dtype), kind="ExternalInput").ap())
    args.append(nc.dram_tensor("out_0_dram", (16, 128, 128), _mybir.dt.float32, kind="ExternalOutput").ap())
    tower_kernel(nc, *args)
    r = _run(nc, [arrays], core_ids=[0])
    return r.results[0]["out_0_dram"]
```
